# Optimizing a Trainium2 kernel written in Bass

```python
import numpy as np
import jax
import jax.numpy as jnp

def _softmax(x, axis=-1):
    return jax.nn.softmax(x, axis=axis)

def _gelu(x):
    return jax.nn.gelu(x, approximate=True)

def _silu(x):
    return jax.nn.silu(x)

def _sigmoid(x):
    return jax.nn.sigmoid(x)

def _layernorm(x, axis=-1, eps=1e-05):
    m = jnp.mean(x, axis=axis, keepdims=True)
    v = jnp.var(x, axis=axis, keepdims=True)
    return (x - m) / jnp.sqrt(v + eps)

def _scatter_add(tgt, idx, src, axis=0):
    return tgt.at[idx].add(src)

def _segment_sum(src, seg, n):
    return jax.ops.segment_sum(src, seg, n)
kernel_name = 'mk_cond_resid_d4_seqx_r2_44e292'

def setup_inputs(seed: int=0):
    np.random.seed(seed)
    _w = jnp.asarray

    def _rec_inputs():
        import jax
        import jax.numpy as jnp
        _rk = jax.random.key(seed)
        x = -0.000125 + 0.9999 * jax.random.normal(jax.random.fold_in(_rk, 1), (16, 512, 512), jnp.float32)
        _lenS = 512 - jax.random.randint(jax.random.fold_in(_rk, 7), (16,), 0, max(1, 512 // 4) + 1, jnp.int32)
        _lenS2 = 512 - jax.random.randint(jax.random.fold_in(_rk, 8), (16,), 0, max(1, 512 // 4) + 1, jnp.int32)
        cond_1024 = -0.00493535 + 1.00056 * jax.random.normal(jax.random.fold_in(_rk, 11), (16, 512), jnp.float32)
        return (x, cond_1024)
    x, cond_1024 = _rec_inputs()

    def _L0_cond_setup():
        import jax, jax.numpy as jnp
        import numpy as np
        import math
        D = 512
        H = 512
        key = jax.random.key(seed)
        k1, k2, k3, k4 = jax.random.split(key, 4)
        x = jax.random.normal(k1, (64, 256, D), dtype=jnp.float32)
        h0 = jax.random.normal(k2, (64, H), dtype=jnp.float32)
        Wx = jax.random.normal(k3, (D, 4 * H), dtype=jnp.float32) / math.sqrt(D)
        Wh = jax.random.normal(k4, (H, 4 * H), dtype=jnp.float32) / math.sqrt(H)
        b = jnp.zeros((4 * H,), dtype=jnp.float32)
        return {'x': x, 'h0': h0, 'Wx': Wx, 'Wh': Wh, 'b': b}
    _L0_cond_all = _L0_cond_setup()
    _L0_cond_in = {k: v for k, v in _L0_cond_all.items() if k in ('Wx', 'Wh', 'b')}
    del _L0_cond_all

    def _L1_cond_setup():
        import jax, jax.numpy as jnp
        import numpy as np
        key = jax.random.key(seed)
        ks = jax.random.split(key, 8)
        B, L, D, N, K = (4, 2048, 512, 64, 4)
        return {'x': jax.random.normal(ks[0], (B, L, D), dtype=jnp.float32), 'conv_w': jax.random.normal(ks[1], (K, 1, D), dtype=jnp.float32) * 0.1, 'conv_b': jnp.zeros((D,), dtype=jnp.float32), 'Wp': jax.random.normal(ks[2], (D, 2 * N), dtype=jnp.float32) * (1.0 / np.sqrt(D)), 'bp': jnp.zeros((2 * N,), dtype=jnp.float32), 'Ws': jax.random.normal(ks[3], (D, N), dtype=jnp.float32) * (1.0 / np.sqrt(D)), 'bs': jnp.zeros((N,), dtype=jnp.float32), 'A_log': jax.random.normal(ks[4], (N,), dtype=jnp.float32) * 0.02, 'dt_log': jax.random.normal(ks[5], (N,), dtype=jnp.float32) * 0.02, 'Wo': jax.random.normal(ks[6], (N, D), dtype=jnp.float32) * (1.0 / np.sqrt(N)), 'bo': jnp.zeros((D,), dtype=jnp.float32)}
    _L1_cond_all = _L1_cond_setup()
    _L1_cond_in = {k: v for k, v in _L1_cond_all.items() if k in ('conv_b', 'Wp', 'bp', 'Ws', 'bs', 'A_log', 'dt_log', 'Wo', 'bo')}
    del _L1_cond_all

    def _L2_cond_setup():
        import jax, jax.numpy as jnp
        import numpy as np
        B, T, D = (128, 32, 512)
        ADA, INTER, RANK = (512, 512, 8)
        LN_EPS = 1e-05

        def _layernorm(x, g, b):
            mu = jnp.mean(x, axis=-1, keepdims=True)
            var = jnp.var(x, axis=-1, keepdims=True)
            return (x - mu) * jax.lax.rsqrt(var + LN_EPS) * g + b
        key = jax.random.key(seed)
        ks = jax.random.split(key, 9)
        return {'x': jax.random.normal(ks[0], (B, T, D), dtype=jnp.float32), 'ada_emb': jax.random.normal(ks[1], (B, ADA), dtype=jnp.float32), 'base_layer': jax.random.normal(ks[2], (D, D), dtype=jnp.float32), 'w1': jax.random.normal(ks[3], (ADA, INTER), dtype=jnp.float32) * 0.02, 'b1': jnp.zeros((INTER,), dtype=jnp.float32), 'w2': jax.random.normal(ks[4], (INTER, 2 * D * RANK), dtype=jnp.float32) * 0.02, 'b2': jnp.zeros((2 * D * RANK,), dtype=jnp.float32), 'ln_g': jnp.ones((ADA,), dtype=jnp.float32), 'ln_b': jnp.zeros((ADA,), dtype=jnp.float32)}
    _L2_cond_all = _L2_cond_setup()
    _L2_cond_in = {k: v for k, v in _L2_cond_all.items() if k in ('base_layer', 'w1', 'b1', 'w2', 'b2', 'ln_g', 'ln_b')}
    del _L2_cond_all

    def _L3_cond_setup():
        import jax, jax.numpy as jnp
        import numpy as np
        LATENT = 512
        key = jax.random.key(seed)
        k1, k2, k3, k4 = jax.random.split(key, 4)
        B, T, D = (64, 256, LATENT)
        h_t = jax.random.normal(k1, (B, D), dtype=jnp.float32)
        z = jax.random.normal(k2, (B, T, D), dtype=jnp.float32)
        bound = 1.0 / np.sqrt(2 * D)
        W = jax.random.uniform(k3, (D, 2 * D), minval=-bound, maxval=bound, dtype=jnp.float32)
        b = jax.random.uniform(k4, (D,), minval=-bound, maxval=bound, dtype=jnp.float32)
        alpha = jnp.full((D,), 0.1, dtype=jnp.float32)
        return {'h_t': h_t, 'z': z, 'W': W, 'b': b, 'alpha': alpha}
    _L3_cond_all = _L3_cond_setup()
    _L3_cond_in = {k: v for k, v in _L3_cond_all.items() if k in ('W', 'b', 'alpha')}
    del _L3_cond_all
    return {'x': x, 'cond_1024': cond_1024, 'L0_cond_Wx': _L0_cond_in['Wx'], 'L0_cond_Wh': _L0_cond_in['Wh'], 'L0_cond_b': _L0_cond_in['b'], 'L1_cond_conv_b': _L1_cond_in['conv_b'], 'L1_cond_Wp': _L1_cond_in['Wp'], 'L1_cond_bp': _L1_cond_in['bp'], 'L1_cond_Ws': _L1_cond_in['Ws'], 'L1_cond_bs': _L1_cond_in['bs'], 'L1_cond_A_log': _L1_cond_in['A_log'], 'L1_cond_dt_log': _L1_cond_in['dt_log'], 'L1_cond_Wo': _L1_cond_in['Wo'], 'L1_cond_bo': _L1_cond_in['bo'], 'L2_cond_base_layer': _L2_cond_in['base_layer'], 'L2_cond_w1': _L2_cond_in['w1'], 'L2_cond_b1': _L2_cond_in['b1'], 'L2_cond_w2': _L2_cond_in['w2'], 'L2_cond_b2': _L2_cond_in['b2'], 'L2_cond_ln_g': _L2_cond_in['ln_g'], 'L2_cond_ln_b': _L2_cond_in['ln_b'], 'L3_cond_W': _L3_cond_in['W'], 'L3_cond_b': _L3_cond_in['b'], 'L3_cond_alpha': _L3_cond_in['alpha']}

def reference(x, cond_1024, L0_cond_Wx, L0_cond_Wh, L0_cond_b, L1_cond_conv_b, L1_cond_Wp, L1_cond_bp, L1_cond_Ws, L1_cond_bs, L1_cond_A_log, L1_cond_dt_log, L1_cond_Wo, L1_cond_bo, L2_cond_base_layer, L2_cond_w1, L2_cond_b1, L2_cond_w2, L2_cond_b2, L2_cond_ln_g, L2_cond_ln_b, L3_cond_W, L3_cond_b, L3_cond_alpha):
    import jax
    import jax.numpy as jnp

    def _L0_cond_ref(x, h0, Wx, Wh, b):
        import jax, jax.numpy as jnp
        import numpy as np
        import math
        D = 512
        H = 512
        Hdim = h0.shape[1]
        xW = jnp.einsum('ntd,dk->ntk', x, Wx) + b
        c0 = jnp.zeros_like(h0)

        def step(carry, xw_t):
            prev_h, prev_c = carry
            a = xw_t + prev_h @ Wh
            i = jax.nn.sigmoid(a[:, :Hdim])
            f = jax.nn.sigmoid(a[:, Hdim:2 * Hdim])
            o = jax.nn.sigmoid(a[:, 2 * Hdim:3 * Hdim])
            g = jnp.tanh(a[:, 3 * Hdim:])
            next_c = f * prev_c + i * g
            next_h = o * jnp.tanh(next_c)
            return ((next_h, next_c), next_h)
        xW_t = jnp.swapaxes(xW, 0, 1)
        _, hs = jax.lax.scan(step, (h0, c0), xW_t)
        hn = jnp.swapaxes(hs, 0, 1)
        return hn

    def _L1_cond_ref(x, conv_w, conv_b, Wp, bp, Ws, bs, A_log, dt_log, Wo, bo):
        import jax, jax.numpy as jnp
        import numpy as np
        B, L, D = x.shape
        K = conv_w.shape[0]
        N = Ws.shape[1]
        x_pad = jnp.pad(x, ((0, 0), (K - 1, 0), (0, 0)))
        conv = conv_b + sum((x_pad[:, k:k + L, :] * conv_w[k, 0] for k in range(K)))
        proj = conv @ Wp + bp
        B_t = jax.nn.softplus(proj[..., :N])
        C_t = jnp.tanh(proj[..., N:])
        u = x @ Ws + bs
        A = -jax.nn.softplus(A_log)
        dt = jax.nn.softplus(dt_log)
        decay = 1.0 + dt * A

        def step(state, inputs):
            u_t, b_t, c_t = inputs
            state = decay * state + dt * b_t * u_t
            return (state, c_t * state)
        init = jnp.zeros((B, N), dtype=x.dtype)
        xs = tuple((jnp.swapaxes(a, 0, 1) for a in (u, B_t, C_t)))
        _, ys = jax.lax.scan(step, init, xs, unroll=4)
        y = jnp.swapaxes(ys, 0, 1)
        return y @ Wo + bo

    def _L2_cond_ref(x, ada_emb, base_layer, w1, b1, w2, b2, ln_g, ln_b):
        import jax, jax.numpy as jnp
        import numpy as np
        B, T, D = (128, 32, 512)
        ADA, INTER, RANK = (512, 512, 8)
        LN_EPS = 1e-05

        def _layernorm(x, g, b):
            mu = jnp.mean(x, axis=-1, keepdims=True)
            var = jnp.var(x, axis=-1, keepdims=True)
            return (x - mu) * jax.lax.rsqrt(var + LN_EPS) * g + b
        b, t, d = x.shape
        ae = _layernorm(ada_emb, ln_g, ln_b)
        h = jax.nn.gelu(ae @ w1 + b1, approximate=False)
        xw = h @ w2 + b2
        x_a, x_b = jnp.split(xw, 2, axis=-1)
        x_a = x_a.reshape(b, d, RANK)
        x_b = x_b.reshape(b, d, RANK)
        layer = base_layer[None, :, :] + jnp.einsum('bdr,bkr->bdk', x_a, x_b)
        out = jnp.einsum('btc,bco->bto', x, layer)
        return x + out

    def _L3_cond_ref(h_t, z, W, b, alpha):
        import jax, jax.numpy as jnp
        import numpy as np
        LATENT = 512
        D = h_t.shape[-1]
        Wh = W[:, :D]
        Wz = W[:, D:]
        leak = 1.0 - alpha

        def step(h, z_t):
            gate = jax.nn.sigmoid(h @ Wh.T + z_t @ Wz.T + b)
            h_new = jnp.tanh(h * leak + gate * z_t)
            return (h_new, h_new)
        _, hs = jax.lax.scan(step, h_t, jnp.swapaxes(z, 0, 1))
        return jnp.swapaxes(hs, 0, 1)
    x = x + _L0_cond_ref(x, cond_1024, L0_cond_Wx, L0_cond_Wh, L0_cond_b)
    x = x + _L1_cond_ref(x, cond_1024[:, None, :], L1_cond_conv_b, L1_cond_Wp, L1_cond_bp, L1_cond_Ws, L1_cond_bs, L1_cond_A_log, L1_cond_dt_log, L1_cond_Wo, L1_cond_bo)
    x = x + _L2_cond_ref(x, cond_1024, L2_cond_base_layer, L2_cond_w1, L2_cond_b1, L2_cond_w2, L2_cond_b2, L2_cond_ln_g, L2_cond_ln_b)
    x = x + _L3_cond_ref(cond_1024, x, L3_cond_W, L3_cond_b, L3_cond_alpha)
    return x

_drawn_inputs = setup_inputs


def setup_inputs(seed=0):
    import zlib

    import numpy as np

    out = dict(_drawn_inputs(seed))
    spreads = {'L0_cond_b': (0.0, 0.1),
     'L1_cond_conv_b': (0.0, 0.1),
     'L1_cond_bp': (0.0, 0.1),
     'L1_cond_bs': (0.0, 0.1),
     'L1_cond_bo': (0.0, 0.1),
     'L2_cond_b1': (0.0, 0.458),
     'L2_cond_b2': (0.0, 0.1),
     'L2_cond_ln_g': (1.0, 0.6),
     'L2_cond_ln_b': (0.0, 0.8),
     'L3_cond_alpha': (0.10000000149011612, 0.6)}
    factors = {'L1_cond_A_log': 5.991, 'L1_cond_dt_log': 4.145, 'L3_cond_W': 5.131, 'L3_cond_b': 8.0}
    for name, (base, spread) in spreads.items():
        noise = np.random.default_rng([zlib.crc32(name.encode()), seed]).standard_normal(out[name].shape)
        drawn = base * np.exp(spread * noise) if base else spread * noise
        out[name] = jnp.asarray(drawn.astype(out[name].dtype))
    for name, factor in factors.items():
        out[name] = (out[name] * factor).astype(out[name].dtype)
    return out
```

```python
import concourse.bass as bass
from concourse import mybir
from contextlib import ExitStack

B = 16
T = 512
D = 512
P = 128
KT = D // P
S = 16
C = S * B
NCH = T // S
NG = 4 * D // P
NGIF = 3 * D // P
GIF = NGIF * B
W1 = KT * B
N = 64
TAPS = 16
R = 8
LAG = 4
EPS = 1e-5
PIECE = 4096
HALO = (TAPS - 1) * B

SMALL = {}
_at = 0
for _name, _n in (("cond", W1), ("b0", NG), ("conv_b", KT), ("bo", KT), ("b3", KT), ("b1", KT), ("ln_g", KT),
                  ("ln_b", KT), ("b2", 2 * KT * R), ("alpha", W1), ("bp", 1), ("bs", 1), ("a_dt", 2),
                  ("mask", C), ("ident", P)):
    SMALL[_name] = slice(_at, _at + _n)
    _at += _n
NSMALL = _at

DVE_VAR, DVE_NORM = 3, 5
DVE_AE = DVE_NORM + KT
DVE_LORA = 26
SETUP_DVE = DVE_LORA + 3 * KT + KT + 2
PE_HIDDEN = 2
CONV_OPS = TAPS * KT
CONV_PER = 9
SCAN_OPS = 9
XW_FIRST = 3
XW_COUNT = {3: 2, 4: 1, 5: 2, 6: 2, 7: 2, 8: 2, 9: 1, 10: 2, 11: 1, 12: 1}
XW_AT, _at = [], 0
for _s in range(S):
    XW_AT.append(range(_at, _at + XW_COUNT.get(_s, 0)))
    _at += XW_COUNT.get(_s, 0)
assert _at == NG


def lora_read(t):
    return DVE_LORA + (3 * t if t < KT else 2 * KT + t) + 1


N_PIECES = 7 + 2 * KT


def cond_resid_kernel(nc, xT, cond_row, small, pieces, outT):
    f32 = mybir.dt.float32
    bf16 = mybir.dt.bfloat16
    ALU = mybir.AluOpType
    ACT = mybir.ActivationFunctionType

    ctx = ExitStack()
    with ctx:
        def sb(name, cols, dt=f32, parts=P):
            return ctx.enter_context(nc.sbuf_tensor(name, [parts, cols], dt))

        def sem(name):
            return ctx.enter_context(nc.semaphore(name))

        wh = [sb(f"wh_{p}", KT * 4 * D, bf16) for p in ("hi", "lo")]
        wx = [sb(f"wx_{p}", KT * 4 * D, bf16) for p in ("hi", "lo")]
        m1 = [sb(f"base_wz_{p}", 2 * KT * D, bf16) for p in ("hi", "lo")]
        m2 = [sb(f"wg_wp_ws_wo_{p}", PIECE, bf16) for p in ("hi", "lo")]
        lra = [sb(f"lora_a_{p}", KT * P, bf16) for p in ("hi", "lo")]
        lrb = [sb(f"lora_b_{p}", D, bf16) for p in ("hi", "lo")]

        def whs(p, kt, ft):
            return wh[p][:, (kt * NG + ft) * P:(kt * NG + ft + 1) * P]

        def wxs(p, kt, ft):
            return wx[p][:, (kt * NG + ft) * P:(kt * NG + ft + 1) * P]

        def bases(p, kt, ot):
            return m1[p][:, kt * D + ot * P:kt * D + (ot + 1) * P]

        def wzs(p, kt, ot):
            return m1[p][:, (KT + kt) * D + ot * P:(KT + kt) * D + (ot + 1) * P]

        def wgs(p, kt, ot):
            return m2[p][:, kt * D + ot * P:kt * D + (ot + 1) * P]

        def wps(p, kt):
            return m2[p][:, KT * D + kt * P:KT * D + (kt + 1) * P]

        def wss(p, kt):
            return m2[p][:, KT * D + D + kt * P:KT * D + D + (kt + 1) * P]

        def wos(p, ot):
            return m2[p][0:N, KT * D + 2 * D + ot * P:KT * D + 2 * D + (ot + 1) * P]

        sp = sb("small_params", NSMALL)

        def par(name, k=None):
            a = SMALL[name]
            return sp[:, a] if k is None else sp[:, a.start + k:a.start + k + 1]

        leak = sb("leak", W1)
        ssm = sb("ssm_params", 8, parts=N)
        decay_t = sb("decay_tile", C, parts=N)

        xw = sb("xw", 2 * S * NG * B)
        x_in = sb("x_in", KT * C)
        x_s = [sb(f"x_{p}", KT * C, bf16) for p in ("hi", "lo")]
        x_res = sb("x_res", KT * C)
        x1 = sb("x1", KT * C)
        win = sb("win", KT * (HALO + C))
        conv = sb("conv", KT * C)
        conv_s = [sb(f"conv_{p}", KT * C, bf16) for p in ("hi", "lo")]
        win_s = conv_s
        x2, x2_s = conv, conv_s
        x3 = sb("x3", KT * C)
        x3_s = [sb(f"x3_{p}", KT * C, bf16) for p in ("hi", "lo")]
        zw = sb("zw", KT * C)
        z_c = sb("z_cur", S * W1)
        zw_c = sb("zw_cur", S * W1)
        outb = sb("outb", KT * C)
        gsum = sb("gate_sums", NG * B)
        fi = sb("sig_f_i", 2 * W1)
        cg = sb("c_and_g", 2 * W1)
        fcig = sb("fc_ig", 2 * W1)
        so = sb("sig_o", W1)
        tc = sb("tanh_c", W1)
        h0 = sb("h0", W1)
        h0_s = sb("h0_split", 2 * W1, bf16)
        s3 = sb("l3_sums", W1)
        gate3 = sb("l3_gate", W1)
        gz = sb("l3_gz", W1)
        hl = sb("l3_h_leak", W1)
        pre3 = sb("l3_pre", W1)
        h3 = sb("l3_h", W1)
        h3_s = sb("l3_h_split", 2 * W1, bf16)
        spa = sb("sp_terms", C, parts=N)
        spe = spl = spa
        spr = sb("sp_relu", C, parts=N)
        bt = sb("b_t", C, parts=N)
        ct = sb("c_t", C, parts=N)
        bu = sb("b_u", C, parts=N)
        vbt = sb("v_bt", C, parts=N)
        state = sb("state", C, parts=N)
        y = sb("y", C, parts=N)
        y_s = [sb(f"y_{p}", C, bf16, parts=N) for p in ("hi", "lo")]
        vm = sb("lora_v", C)
        v_s = [sb(f"lora_v_{p}", C, bf16) for p in ("hi", "lo")]
        crow = outb[0:B, 0:D]
        stats = sb("ln_stats", 16, parts=B)
        ae = x1
        hid = x2
        lrt = x3

        def pb(name):
            return ctx.enter_context(nc.psum_tensor(name, [P, 512], f32))

        p_gif, p_o, p_l3, p_x0, p_x1, p_m0, p_m1, p_p = (
            pb(n) for n in ("p_gif", "p_o", "p_l3", "p_x0", "p_x1", "p_m0", "p_m1", "p_proj"))
        p_x = [p_x0, p_x1]
        p_m = [p_m0, p_m1]

        small_in, piece_in = sem("small_in"), [sem("piece_in_even"), sem("piece_in_odd")]
        piece_split = sem("piece_split")
        x_loaded, res_loaded, out_stored = sem("x_loaded"), sem("res_loaded"), sem("out_stored")
        setup_dve, setup_act, setup_pe = sem("setup_dve"), sem("setup_act"), sem("setup_pe")
        x_split_hi, x_split_lo = sem("x_split_hi"), sem("x_split_lo")
        xw_mm, xw_done = sem("xw_mm"), sem("xw_done")
        gif_mm, o_mm = sem("gif_mm"), sem("o_mm")
        gif_part, gif_sum, o_part, o_sum = sem("gif_part"), sem("gif_sum"), sem("o_part"), sem("o_sum")
        g_tanh, fi_sig, o_sig, c_tanh = sem("g_tanh"), sem("fi_sig"), sem("o_sig"), sem("c_tanh")
        fcig_done, c_new, h0_f32, h0_split, x1_done = (sem(n) for n in ("fcig_done", "c_new", "h0_f32", "h0_split", "x1_done"))
        win_moved, win_hi, win_lo, u_mm, conv_op, conv_hi, conv_lo, proj_mm = (
            sem(n) for n in ("win_moved", "win_hi", "win_lo", "u_mm", "conv_op", "conv_hi", "conv_lo", "proj_mm"))
        sp_abs, c_done, sp_exp, sp_log, scan_op, wo_mm, x2_done, x2_hi, x2_lo = (
            sem(n) for n in ("sp_abs_done", "c_done", "sp_exp_done", "sp_log_done", "scan_op", "wo_mm", "x2_done",
                             "x2_hi_done", "x2_lo_done"))
        v_mm, v_op, l2_mm, x3_done, x3_hi, x3_lo, zw_mm, zw_done, z_moved = (
            sem(n) for n in ("v_mm", "v_op", "l2_mm", "x3_done", "x3_hi_done", "x3_lo_done", "zw_mm", "zw_done", "z_moved"))
        l3_mm, s3_part, s3_sum, l3_gate, l3_gz, l3_pre, l3_h, l3_split, l3_leak, l3_out = (
            sem(n) for n in ("l3_mm", "s3_part", "s3_sum", "l3_gate_done", "l3_gz_done", "l3_pre_done", "l3_h_done",
                             "l3_split", "l3_leak_done", "l3_out_done"))

        def kb(t, lo, n=W1):
            return t[:, lo:lo + n].rearrange("p (k b) -> p k b", b=B)

        def step_cols(t, s):
            return t[:, :].rearrange("p (k c) -> p k c", k=KT)[:, :, s * B:(s + 1) * B]

        def tile(t, k):
            return t[:, k * C:(k + 1) * C]

        def xw_slots(p):
            return xw[:, bass.ds(p * (S * NG * B), S * NG * B)].rearrange("p (t g) -> p t g", t=S)

        def xw_step(p, s):
            return xw[:, bass.ds(p * (S * NG * B) + s * NG * B, NG * B)].rearrange("p (g b) -> p g b", b=B)

        win_v = win[:, :].rearrange("p (k c) -> p k c", k=KT)
        x1_v = x1[:, :].rearrange("p (k c) -> p k c", k=KT)
        h0_v = h0_s[:, :].rearrange("p (k q b) -> p k q b", q=2, b=B)
        h3_v = h3_s[:, :].rearrange("p (k q b) -> p k q b", q=2, b=B)

        block = ctx.enter_context(nc.Block())

        def has_l0(c):
            return not isinstance(c, int) or c < NCH

        def has_mid(c):
            return not isinstance(c, int) or 1 <= c <= NCH

        def has_z(c):
            return not isinstance(c, int) or 2 <= c <= NCH + 1

        def has_l3(c, s):
            return not isinstance(c, int) or 0 <= S * (c - 2) + s - LAG < T

        def iterations(engine, body):
            for c in (0, 1, 2):
                body(c)
            with engine.Fori(3, NCH) as c:
                body(c)
            for c in (NCH, NCH + 1, NCH + 2):
                body(c)

        @block.sync
        def _(sync):
            sync.dma_start(sp[:, :], small).then_inc(small_in, 16)
            sync.dma_start(crow, cond_row).then_inc(small_in, 16)
            sync.dma_start(x_in[:, :], xT[0, :, :]).then_inc(x_loaded, 16)
            for n in range(N_PIECES):
                if 2 <= n < 8:
                    sync.wait_ge(piece_split, n - 1)
                elif n >= 8:
                    sync.wait_ge(setup_pe, PE_HIDDEN + n - 8)
                sync.dma_start(xw[:, (n % 2) * PIECE:(n % 2 + 1) * PIECE], pieces[n, :, :]).then_inc(piece_in[n % 2], 16)

            def body(c):
                if has_l0(c):
                    sync.wait_ge(x_split_hi, c + 1)
                    sync.wait_ge(x_split_lo, c + 1)
                    sync.dma_start(x_in[:, :], xT[c + 1, :, :]).then_inc(x_loaded, 16)
                    if not (isinstance(c, int) and c == 0):
                        sync.wait_ge(x1_done, S * c)
                    sync.dma_start(x_res[:, :], xT[c, :, :]).then_inc(res_loaded, 16)
                if not isinstance(c, int) or c >= 3:
                    sync.wait_ge(l3_out, S * (c - 2))
                    sync.dma_start(outT[c - 3, :, :], outb[:, :]).then_inc(out_stored, 16)

            iterations(sync, body)
            sync.wait_ge(out_stored, 16 * NCH)
            sync.wait_ge(x_loaded, 16 * (NCH + 1))

        @block.gpsimd
        def _(pool):
            def low(dst, src, hi, done, ready, n):
                pool.wait_ge(ready, n)
                nc.gpsimd.tensor_tensor(dst, src, hi, ALU.subtract).then_inc(done, 1)

            low(x_s[1][:, :], x_in[:, :], x_s[0][:, :], x_split_lo, x_split_hi, 1)

            def body(c):
                m = c - 1
                for s in range(S):
                    g3 = S * (c - 2) + s - LAG
                    if s == 0 and has_l0(c):
                        low(x_s[1][:, :], x_in[:, :], x_s[0][:, :], x_split_lo, x_split_hi, c + 2)
                    if s == 0 and has_z(c):
                        low(x3_s[1][:, :], x3[:, :], x3_s[0][:, :], x3_lo, x3_hi, c - 1)
                    if s == 1 and has_mid(c):
                        pool.wait_ge(win_hi, c)
                        nc.gpsimd.tensor_tensor(win_s[1][:, :].rearrange("p (k c) -> p k c", k=KT), win_v[:, :, HALO:],
                                                win_s[0][:, :].rearrange("p (k c) -> p k c", k=KT),
                                                ALU.subtract).then_inc(win_lo, 1)
                    if s == 8 and has_mid(c):
                        low(conv_s[1][:, :], conv[:, :], conv_s[0][:, :], conv_lo, conv_hi, c)
                    if s == 12 and has_mid(c):
                        low(x2_s[1][:, :], x2[:, :], x2_s[0][:, :], x2_lo, x2_hi, c)
                    if has_l3(c, s):
                        if not (isinstance(c, int) and c == 2 and s == LAG):
                            pool.wait_ge(l3_h, g3)
                            pool.wait_ge(l3_pre, g3)
                        else:
                            pool.wait_ge(setup_dve, SETUP_DVE)
                        nc.gpsimd.tensor_tensor(hl[:, :], h3[:, :], leak[:, :], ALU.mult).then_inc(l3_leak, 1)
                        if s == LAG and not (isinstance(c, int) and c == 2):
                            pool.wait_ge(out_stored, 16 * (c - 2))
                        pool.wait_ge(l3_h, g3 + 1)
                        t = (s - LAG) % S
                        nc.gpsimd.tensor_tensor(step_cols(outb, t), kb(z_c, t * W1), kb(h3, 0), ALU.add).then_inc(l3_out, 1)

            iterations(pool, body)

        SETUP_ACT = {}

        @block.scalar
        def _(act):
            done = [0]

            def setup(name, ins):
                ins.then_inc(setup_act, 1)
                done[0] += 1
                SETUP_ACT[name] = done[0]

            act.wait_ge(small_in, 32)
            setup("abs", nc.scalar.activation(ssm[:, 3:5], par("a_dt")[0:N, :], ACT.Abs))
            act.wait_ge(setup_act, 1)
            setup("exp", nc.scalar.activation(ssm[:, 5:7], ssm[:, 3:5], ACT.Exp, scale=-1.0))
            act.wait_ge(setup_act, 2)
            setup("log", nc.scalar.activation(ssm[:, 3:5], ssm[:, 5:7], ACT.Ln, bias=1.0))
            act.wait_ge(setup_dve, DVE_VAR)
            setup("std", nc.scalar.activation(stats[:, 9:10], stats[:, 8:9], ACT.Sqrt))
            act.wait_ge(setup_pe, 2)
            for it in range(KT):
                setup("gelu", nc.scalar.activation(hid[:, it * B:(it + 1) * B], p_p[:, 64 + it * B:64 + (it + 1) * B],
                                                   ACT.Gelu, bias=par("b1", it)))

            def high(dst, src, done, ready, n):
                act.wait_ge(ready, n)
                nc.scalar.activation(dst, src, ACT.Copy).then_inc(done, 1)

            def xw_out(q, par_, ft):
                act.wait_ge(xw_mm, NG * q + ft + 1)
                out = xw_slots(par_)[:, :, ft * B:(ft + 1) * B]
                nc.scalar.activation(out, p_x[ft % 2][:, 0:C].rearrange("p (t b) -> p t b", b=B), ACT.Identity,
                                     bias=par("b0", ft)).then_inc(xw_done, 1)

            high(x_s[0][:, :], x_in[:, :], x_split_hi, x_loaded, 16)
            act.wait_ge(setup_pe, PE_HIDDEN + 2 * KT)
            for ft in range(NG):
                xw_out(0, 0, ft)

            def body(c):
                for s in range(S):
                    g = S * c + s
                    g3 = S * (c - 2) + s - LAG
                    if s == 0 and has_l0(c):
                        act.wait_ge(xw_mm, NG * (c + 1))
                        high(x_s[0][:, :], x_in[:, :], x_split_hi, x_loaded, 16 * (c + 2))
                    if s == 0 and has_z(c):
                        high(x3_s[0][:, :], x3[:, :], x3_hi, x3_done, KT * (c - 1))
                    if has_l0(c):
                        act.wait_ge(gif_sum, g + 1)
                        nc.scalar.activation(cg[:, W1:2 * W1], gsum[:, 0:W1], ACT.Tanh).then_inc(g_tanh, 1)
                        nc.scalar.activation(fi[:, :], gsum[:, W1:3 * W1], ACT.Sigmoid).then_inc(fi_sig, 1)
                        act.wait_ge(o_sum, g + 1)
                        nc.scalar.activation(so[:, :], gsum[:, 3 * W1:4 * W1], ACT.Sigmoid).then_inc(o_sig, 1)
                        act.wait_ge(c_new, g + 1)
                        nc.scalar.activation(tc[:, :], cg[:, 0:W1], ACT.Tanh).then_inc(c_tanh, 1)
                    if has_l3(c, s):
                        act.wait_ge(s3_sum, g3 + 1)
                        nc.scalar.activation(gate3[:, :], s3[:, :], ACT.Sigmoid).then_inc(l3_gate, 1)
                        act.wait_ge(l3_pre, g3 + 1)
                        if not (isinstance(c, int) and c == 2 and s == LAG):
                            act.wait_ge(l3_split, 2 * g3 + 2)
                            act.wait_ge(l3_out, g3)
                        act.wait_ge(l3_leak, g3 + 1)
                        nc.scalar.activation(h3[:, :], pre3[:, :], ACT.Tanh).then_inc(l3_h, 1)
                    if s == 0 and has_mid(c):
                        act.wait_ge(win_moved, 2 * c)
                        nc.scalar.activation(win_s[0][:, :].rearrange("p (k c) -> p k c", k=KT), win_v[:, :, HALO:],
                                             ACT.Copy).then_inc(win_hi, 1)
                    if s == 7 and has_mid(c):
                        high(conv_s[0][:, :], conv[:, :], conv_hi, conv_op, CONV_OPS * c)
                    if s == 9 and has_mid(c):
                        act.wait_ge(proj_mm, c)
                        nc.scalar.activation(spa[:, :], p_p[0:N, 0:C], ACT.Abs, bias=par("bp")[0:N, :]).then_inc(sp_abs, 1)
                        nc.scalar.activation(ct[:, :], p_p[N:P, 0:C], ACT.Tanh, bias=par("bp")[N:P, :]).then_inc(c_done, 1)
                        act.wait_ge(sp_abs, c)
                        nc.scalar.activation(spe[:, :], spa[:, :], ACT.Exp, scale=-1.0).then_inc(sp_exp, 1)
                        act.wait_ge(sp_exp, c)
                        nc.scalar.activation(spl[:, :], spe[:, :], ACT.Ln, bias=1.0).then_inc(sp_log, 1)
                    if s == 11 and has_mid(c):
                        high(x2_s[0][:, :], x2[:, :], x2_hi, x2_done, KT * c)
                    if s in (2, 3) and has_z(c):
                        for ot in (2 * (s - 2), 2 * (s - 2) + 1):
                            act.wait_ge(zw_mm, KT * (c - 2) + 2 * (s - 2) + 2)
                            nc.scalar.activation(tile(zw, ot), p_m[ot // 2][:, (ot % 2) * C:(ot % 2 + 1) * C], ACT.Identity,
                                                 bias=par("b3", ot)).then_inc(zw_done, 1)
                    if has_l0(c):
                        for ft in XW_AT[s]:
                            xw_out(c + 1, (c + 1) % 2, ft)

            iterations(act, body)

        @block.tensor
        def _(pe):
            mm = nc.tensor.matmul

            def three(out, ws, xs, kts, first, last):
                todo = [(k, a, b) for k in kts for a, b in ((0, 0), (0, 1), (1, 0))]
                ins = None
                for n, (k, a, b) in enumerate(todo):
                    ins = mm(out, ws(a, k), xs(b, k), start=first and n == 0, stop=last and n == len(todo) - 1)
                return ins

            pe.wait_ge(setup_dve, DVE_NORM)
            for k in range(KT):
                ins = nc.tensor.transpose(p_p[:, k * B:(k + 1) * B], outb[0:B, k * P:(k + 1) * P], par("ident")[0:B, 0:B])
            ins.then_inc(setup_pe, 1)
            pe.wait_ge(piece_in[0], 16 * 4)
            pe.wait_ge(setup_dve, DVE_AE)
            for it in range(KT):
                for k in range(KT):
                    ins = mm(p_p[:, 64 + it * B:64 + (it + 1) * B], xw[:, k * D + it * P:k * D + (it + 1) * P],
                             ae[:, k * B:(k + 1) * B], start=k == 0, stop=k == KT - 1)
            ins.then_inc(setup_pe, 1)
            pe.wait_ge(setup_act, SETUP_ACT["gelu"])
            for t in range(2 * KT):
                n = 7 + t
                pe.wait_ge(piece_in[n % 2], 16 * (n // 2 + 1))
                if t >= 2:
                    pe.wait_ge(setup_dve, lora_read(t - 2))
                for r in range(R):
                    for k in range(KT):
                        ins = mm(p_m[t % 2][:, r * B:(r + 1) * B],
                                 xw[:, (n % 2) * PIECE + (k * R + r) * P:(n % 2) * PIECE + (k * R + r + 1) * P],
                                 hid[:, k * B:(k + 1) * B], start=k == 0, stop=k == KT - 1)
                ins.then_inc(setup_pe, 1)
            pe.wait_ge(setup_dve, lora_read(2 * KT - 1))
            for t in range(KT):
                ins = nc.tensor.transpose(p_p[:, t * P:(t + 1) * P], lrt[:, t * P:(t + 1) * P], par("ident"))
            ins.then_inc(setup_pe, 1)

            def xw_products(q, ft):
                if isinstance(q, int) and q == 0 and ft < 2:
                    pass
                else:
                    pe.wait_ge(xw_done, NG * q + ft - 1)
                three(p_x[ft % 2][:, 0:C], lambda a, k: wxs(a, k, ft), lambda b, k: tile(x_s[b], k), range(KT),
                      True, True).then_inc(xw_mm, 1)

            def lstm_products(c, s):
                pe.wait_ge(h0_split, 2 * (S * c + s) + 2)
                for ft in range(NG):
                    bank, at = (p_gif, ft) if ft < NGIF else (p_o, ft - NGIF)
                    for k in range(KT):
                        mm(bank[:, at * 2 * B:(at + 1) * 2 * B], whs(0, k, ft), h0_s[:, k * 2 * B:(k + 1) * 2 * B],
                           start=k == 0, stop=False)
                    for k in range(KT):
                        ins = mm(bank[:, at * 2 * B:at * 2 * B + B], whs(1, k, ft), h0_s[:, k * 2 * B:k * 2 * B + B],
                                 start=False, stop=k == KT - 1)
                    if ft == NGIF - 1:
                        ins.then_inc(gif_mm, 1)
                ins.then_inc(o_mm, 1)

            def l3_products(g3):
                pe.wait_ge(l3_split, 2 * g3 + 2)
                for ot in range(KT):
                    for k in range(KT):
                        mm(p_l3[:, ot * 2 * B:(ot + 1) * 2 * B], wgs(0, k, ot), h3_s[:, k * 2 * B:(k + 1) * 2 * B],
                           start=k == 0, stop=False)
                    for k in range(KT):
                        ins = mm(p_l3[:, ot * 2 * B:ot * 2 * B + B], wgs(1, k, ot), h3_s[:, k * 2 * B:k * 2 * B + B],
                                 start=False, stop=k == KT - 1)
                ins.then_inc(l3_mm, 1)

            pe.wait_ge(piece_split, 6)
            pe.wait_ge(setup_dve, SETUP_DVE)
            pe.wait_ge(x_split_hi, 1)
            pe.wait_ge(x_split_lo, 1)
            for ft in range(NG):
                xw_products(0, ft)

            def body(c):
                for s in range(S):
                    if has_l0(c):
                        lstm_products(c, s)
                    if s in (1, 2) and has_z(c):
                        if s == 1:
                            pe.wait_ge(x3_hi, c - 1)
                            pe.wait_ge(x3_lo, c - 1)
                        for ot in (2 * (s - 1), 2 * (s - 1) + 1):
                            three(p_m[ot // 2][:, (ot % 2) * C:(ot % 2 + 1) * C], lambda a, k: wzs(a, k, ot),
                                  lambda b, k: tile(x3_s[b], k), range(KT), True, True).then_inc(zw_mm, 1)
                    if s == 4 and has_mid(c):
                        pe.wait_ge(win_hi, c)
                        pe.wait_ge(win_lo, c)
                        three(p_p[:, C:2 * C], lambda a, k: wss(a, k), lambda b, k: tile(win_s[b], k), range(KT),
                              True, True).then_inc(u_mm, 1)
                    if s == 9 and has_mid(c):
                        pe.wait_ge(conv_hi, c)
                        pe.wait_ge(conv_lo, c)
                        three(p_p[:, 0:C], lambda a, k: wps(a, k), lambda b, k: tile(conv_s[b], k), range(KT),
                              True, True).then_inc(proj_mm, 1)
                    if s == 11 and has_mid(c):
                        pe.wait_ge(scan_op, SCAN_OPS * c)
                        for ot in range(KT):
                            three(p_m[ot // 2][:, (ot % 2) * C:(ot % 2 + 1) * C], lambda a, k: wos(a, ot),
                                  lambda b, k: y_s[b][:, :], (0,), True, True).then_inc(wo_mm, 1)
                    if s == 13 and has_mid(c):
                        pe.wait_ge(x2_hi, c)
                        pe.wait_ge(x2_lo, c)
                        three(p_p[:, 0:C], lambda a, k: lra[a][:, k * P:(k + 1) * P], lambda b, k: tile(x2_s[b], k),
                              range(KT), True, True).then_inc(v_mm, 1)
                    if s in (14, 15) and has_mid(c):
                        pe.wait_ge(v_op, 3 * c)
                        for ot in (2 * (s - 14), 2 * (s - 14) + 1):
                            out = p_m[ot // 2][:, (ot % 2) * C:(ot % 2 + 1) * C]
                            three(out, lambda a, k: bases(a, k, ot), lambda b, k: tile(x2_s[b], k), range(KT), True, False)
                            three(out, lambda a, k: lrb[a][:, ot * P:(ot + 1) * P], lambda b, k: v_s[b][:, :], (0,),
                                  False, True).then_inc(l2_mm, 1)
                    if has_l0(c) and XW_AT[s]:
                        if s == XW_FIRST:
                            pe.wait_ge(x_split_hi, c + 2)
                            pe.wait_ge(x_split_lo, c + 2)
                        for ft in XW_AT[s]:
                            xw_products(c + 1, ft)
                    if has_l3(c, s):
                        l3_products(S * (c - 2) + s - LAG)

            iterations(pe, body)

        @block.vector
        def _(dve):
            tt, ts, stt = nc.vector.tensor_tensor, nc.vector.tensor_scalar, nc.vector.scalar_tensor_tensor
            n_setup = [0]

            def setup(ins):
                ins.then_inc(setup_dve, 1)
                n_setup[0] += 1

            def settled():
                dve.wait_ge(setup_dve, n_setup[0])

            dve.wait_ge(small_in, 32)
            setup(nc.vector.bn_stats(stats[:, 0:6], crow))
            settled()
            setup(nc.vector.bn_aggr(stats[:, 6:8], stats[:, 0:6]))
            settled()
            setup(ts(stats[:, 8:9], stats[:, 7:8], EPS, None, ALU.add))
            assert n_setup[0] == DVE_VAR
            dve.wait_ge(setup_act, SETUP_ACT["std"])
            setup(nc.vector.reciprocal(stats[:, 10:11], stats[:, 9:10]))
            settled()
            setup(ts(crow, crow, stats[:, 6:7], stats[:, 10:11], ALU.subtract, ALU.mult))
            assert n_setup[0] == DVE_NORM
            dve.wait_ge(setup_pe, 1)
            for k in range(KT):
                setup(ts(ae[:, k * B:(k + 1) * B], p_p[:, k * B:(k + 1) * B], par("ln_g", k), par("ln_b", k),
                         ALU.mult, ALU.add))
            assert n_setup[0] == DVE_AE
            setup(stt(ssm[:, 0:2], par("a_dt")[0:N, :], 0.0, ssm[:, 3:5], ALU.max, ALU.add))
            settled()
            setup(tt(ssm[:, 2:3], ssm[:, 0:1], ssm[:, 1:2], ALU.mult))
            setup(nc.vector.memset(decay_t[:, :], 1.0))
            settled()
            setup(ts(ssm[:, 2:3], ssm[:, 2:3], -1.0, 1.0, ALU.mult, ALU.add))
            setup(nc.vector.memset(decay_t[:, :].rearrange("p (b t) -> p b t", t=S)[:, :, 0], 0.0))
            settled()
            setup(ts(decay_t[:, :], decay_t[:, :], ssm[:, 2:3], None, ALU.mult))
            setup(nc.vector.memset(cg[:, :], 0.0))
            setup(nc.vector.memset(win[:, :], 0.0))
            setup(nc.vector.memset(state[:, :], 0.0))
            setup(ts(leak[:, :], par("alpha"), -1.0, 1.0, ALU.mult, ALU.add))
            setup(nc.vector.tensor_copy(h3[:, :], par("cond")))
            for v, done in ((h0_v, h0_split), (h3_v, l3_split)):
                nc.vector.tensor_copy(v[:, :, 0, :], kb(par("cond"), 0)).then_inc(done, 1)
                dve.wait_ge(done, 1)
                tt(v[:, :, 1, :], kb(par("cond"), 0), v[:, :, 0, :], ALU.subtract).then_inc(done, 1)

            places = [(wh, 0), (wh, PIECE), (wx, 0), (wx, PIECE), (m1, 0), (m2, 0)]
            for n, (dst, at) in enumerate(places):
                src = xw[:, (n % 2) * PIECE:(n % 2 + 1) * PIECE]
                dve.wait_ge(piece_in[n % 2], 16 * (n // 2 + 1))
                setup(nc.vector.tensor_copy(dst[0][:, at:at + PIECE], src))
                settled()
                tt(dst[1][:, at:at + PIECE], src, dst[0][:, at:at + PIECE], ALU.subtract).then_inc(piece_split, 1)
            assert n_setup[0] == DVE_LORA
            for t in range(2 * KT):
                dve.wait_ge(setup_pe, 3 + t)
                if t == KT:
                    settled()
                b2 = sp[:, SMALL["b2"].start + t * R:SMALL["b2"].start + (t + 1) * R]
                out = lrt[:, (t % KT) * P:(t % KT + 1) * P].rearrange("p (b r) -> p r b", r=R)
                setup(tt(out, p_m[t % 2][:, 0:P].rearrange("p (r b) -> p r b", b=B),
                         b2.unsqueeze(2).to_broadcast([P, R, B]), ALU.add))
                settled()
                if t < KT:
                    a = lra[0][:, t * P:(t + 1) * P]
                    setup(nc.vector.tensor_copy(a, lrt[:, t * P:(t + 1) * P]))
                    settled()
                    setup(tt(lra[1][:, t * P:(t + 1) * P], lrt[:, t * P:(t + 1) * P], a, ALU.subtract))
            dve.wait_ge(setup_pe, 3 + 2 * KT)
            setup(nc.vector.tensor_copy(lrb[0][:, :], p_p[:, :]))
            settled()
            setup(tt(lrb[1][:, :], p_p[:, :], lrb[0][:, :], ALU.subtract))
            assert n_setup[0] == SETUP_DVE, n_setup[0]
            settled()

            def conv_tap(c, n):
                j, k = divmod(n, KT)
                base = CONV_OPS * (c - 1)
                src = win[:, k * (HALO + C) + j * B:k * (HALO + C) + j * B + C]
                w = sp[:, SMALL["cond"].start + k * B + j:SMALL["cond"].start + k * B + j + 1]
                if j == 0:
                    ins = ts(tile(conv, k), src, w, par("conv_b", k), ALU.mult, ALU.add)
                else:
                    dve.wait_ge(conv_op, base + n - KT + 1)
                    ins = stt(tile(conv, k), src, w, tile(conv, k), ALU.mult, ALU.add)
                ins.then_inc(conv_op, 1)

            def lstm_step(c, s):
                g = S * c + s
                p = c % 2
                dve.wait_ge(gif_mm, g + 1)
                if s == 0:
                    dve.wait_ge(xw_done, NG * (c + 1))
                    dve.wait_ge(res_loaded, 16 * (c + 1))
                lo = p_gif[:, 0:2 * GIF].rearrange("p (k q b) -> p k q b", q=2, b=B)
                tt(kb(gsum, 0, GIF), lo[:, :, 1, :], xw_step(p, s)[:, 0:NGIF, :], ALU.add).then_inc(gif_part, 1)
                dve.wait_ge(gif_part, g + 1)
                tt(kb(gsum, 0, GIF), lo[:, :, 0, :], kb(gsum, 0, GIF), ALU.add).then_inc(gif_sum, 1)
                dve.wait_ge(o_mm, g + 1)
                lo = p_o[:, 0:2 * W1].rearrange("p (k q b) -> p k q b", q=2, b=B)
                tt(kb(gsum, GIF), lo[:, :, 1, :], xw_step(p, s)[:, NGIF:NG, :], ALU.add).then_inc(o_part, 1)
                dve.wait_ge(o_part, g + 1)
                tt(kb(gsum, GIF), lo[:, :, 0, :], kb(gsum, GIF), ALU.add).then_inc(o_sum, 1)
                dve.wait_ge(g_tanh, g + 1)
                dve.wait_ge(fi_sig, g + 1)
                tt(fcig[:, :], fi[:, :], cg[:, :], ALU.mult).then_inc(fcig_done, 1)
                dve.wait_ge(fcig_done, g + 1)
                tt(cg[:, 0:W1], fcig[:, 0:W1], fcig[:, W1:2 * W1], ALU.add).then_inc(c_new, 1)
                dve.wait_ge(o_sig, g + 1)
                dve.wait_ge(c_tanh, g + 1)
                tt(h0_v[:, :, 0, :], kb(so, 0), kb(tc, 0), ALU.mult).then_inc(h0_split, 1)
                tt(h0[:, :], so[:, :], tc[:, :], ALU.mult).then_inc(h0_f32, 1)
                dve.wait_ge(h0_f32, g + 1)
                dve.wait_ge(h0_split, 2 * g + 3)
                tt(h0_v[:, :, 1, :], kb(h0, 0), h0_v[:, :, 0, :], ALU.subtract).then_inc(h0_split, 1)
                tt(step_cols(x1, s), step_cols(x_res, s), kb(h0, 0), ALU.add).then_inc(x1_done, 1)

            def body(c):
                m = c - 1
                for s in range(S):
                    g3 = S * (c - 2) + s - LAG
                    if s == 0 and has_mid(c):
                        dve.wait_ge(x1_done, S * c)
                        if not (isinstance(c, int) and c == 1):
                            dve.wait_ge(win_lo, c - 1)
                            dve.wait_ge(conv_op, CONV_OPS * (c - 1))
                        nc.vector.tensor_copy(win_v[:, :, 0:HALO], win_v[:, :, C:C + HALO]).then_inc(win_moved, 1)
                        dve.wait_ge(win_moved, 2 * c - 1)
                        nc.vector.tensor_copy(win_v[:, :, HALO:HALO + C], x1_v).then_inc(win_moved, 1)
                    if has_l0(c):
                        lstm_step(c, s)
                    if s == LAG and has_z(c):
                        if not (isinstance(c, int) and c == 2):
                            dve.wait_ge(l3_out, S * (c - 2))
                        nc.vector.tensor_copy(z_c[:, :].rearrange("p (t k b) -> p k t b", k=KT, b=B),
                                              x3[:, :].rearrange("p (k t b) -> p k t b", k=KT, b=B)).then_inc(z_moved, 1)
                        dve.wait_ge(zw_done, KT * (c - 1))
                        nc.vector.tensor_copy(zw_c[:, :].rearrange("p (t k b) -> p k t b", k=KT, b=B),
                                              zw[:, :].rearrange("p (k t b) -> p k t b", k=KT, b=B)).then_inc(z_moved, 1)
                        dve.wait_ge(z_moved, 2 * (c - 1))
                    if s == 0 and has_mid(c):
                        dve.wait_ge(win_moved, 2 * c)
                    conv_now = list(range(CONV_PER * s, min(CONV_PER * (s + 1), CONV_OPS))) if has_mid(c) else []
                    if has_l3(c, s):
                        t = (s - LAG) % S
                        dve.wait_ge(l3_mm, g3 + 1)
                        v = p_l3[:, 0:2 * W1].rearrange("p (k q b) -> p k q b", q=2, b=B)
                        tt(kb(s3, 0), v[:, :, 1, :], kb(zw_c, t * W1), ALU.add).then_inc(s3_part, 1)
                        dve.wait_ge(s3_part, g3 + 1)
                        tt(kb(s3, 0), v[:, :, 0, :], kb(s3, 0), ALU.add).then_inc(s3_sum, 1)
                        for n in conv_now[:2]:
                            conv_tap(c, n)
                        dve.wait_ge(l3_gate, g3 + 1)
                        tt(gz[:, :], gate3[:, :], z_c[:, t * W1:(t + 1) * W1], ALU.mult).then_inc(l3_gz, 1)
                        dve.wait_ge(l3_gz, g3 + 1)
                        dve.wait_ge(l3_leak, g3 + 1)
                        tt(pre3[:, :], gz[:, :], hl[:, :], ALU.add).then_inc(l3_pre, 1)
                        for n in conv_now[2:4]:
                            conv_tap(c, n)
                        dve.wait_ge(l3_h, g3 + 1)
                        nc.vector.tensor_copy(h3_v[:, :, 0, :], kb(h3, 0)).then_inc(l3_split, 1)
                        dve.wait_ge(l3_split, 2 * g3 + 3)
                        tt(h3_v[:, :, 1, :], kb(h3, 0), h3_v[:, :, 0, :], ALU.subtract).then_inc(l3_split, 1)
                        conv_now = conv_now[4:]
                    for n in conv_now:
                        conv_tap(c, n)
                    if s == 10 and has_mid(c):
                        q = SCAN_OPS * (c - 1)
                        dve.wait_ge(sp_abs, c)
                        dve.wait_ge(c_done, c)
                        dve.wait_ge(u_mm, c)
                        ts(spr[:, :], p_p[0:N, 0:C], par("bp")[0:N, :], 0.0, ALU.add, ALU.max).then_inc(scan_op, 1)
                        dve.wait_ge(scan_op, q + 1)
                        dve.wait_ge(sp_log, c)
                        tt(bt[:, :], spr[:, :], spl[:, :], ALU.add).then_inc(scan_op, 1)
                        dve.wait_ge(scan_op, q + 2)
                        stt(bu[:, :], p_p[0:N, C:2 * C], par("bs")[0:N, :], bt[:, :], ALU.add, ALU.mult).then_inc(scan_op, 1)
                        dve.wait_ge(scan_op, q + 3)
                        ts(vbt[:, :].rearrange("p (b t) -> p t b", t=S), bu[:, :].rearrange("p (t b) -> p t b", b=B),
                           ssm[:, 1:2], None, ALU.mult).then_inc(scan_op, 1)
                        dve.wait_ge(scan_op, q + 4)
                        first = vbt[:, :].rearrange("p (b t) -> p b t", t=S)[:, :, 0]
                        last = state[:, :].rearrange("p (b t) -> p b t", t=S)[:, :, S - 1]
                        stt(first, last, ssm[:, 2:3], first, ALU.mult, ALU.add).then_inc(scan_op, 1)
                        dve.wait_ge(scan_op, q + 5)
                        nc.vector.tensor_tensor_scan(state[:, :], decay_t[:, :], vbt[:, :], 0.0, ALU.mult,
                                                     ALU.add).then_inc(scan_op, 1)
                        dve.wait_ge(scan_op, q + 6)
                        tt(y[:, :].rearrange("p (t b) -> p t b", b=B), state[:, :].rearrange("p (b t) -> p t b", t=S),
                           ct[:, :].rearrange("p (t b) -> p t b", b=B), ALU.mult).then_inc(scan_op, 1)
                        dve.wait_ge(scan_op, q + 7)
                        nc.vector.tensor_copy(y_s[0][:, :], y[:, :]).then_inc(scan_op, 1)
                        dve.wait_ge(scan_op, q + 8)
                        tt(y_s[1][:, :], y[:, :], y_s[0][:, :], ALU.subtract).then_inc(scan_op, 1)
                    if s == 11 and has_mid(c):
                        for ot in range(KT):
                            dve.wait_ge(wo_mm, KT * (c - 1) + KT)
                            win_k = win[:, ot * (HALO + C) + HALO:(ot + 1) * (HALO + C)]
                            stt(tile(x2, ot), p_m[ot // 2][:, (ot % 2) * C:(ot % 2 + 1) * C], par("bo", ot), win_k,
                                ALU.add, ALU.add).then_inc(x2_done, 1)
                    if s == 13 and has_mid(c):
                        dve.wait_ge(v_mm, c)
                        base = 3 * (c - 1)
                        tt(vm[:, :], p_p[:, 0:C], par("mask"), ALU.mult).then_inc(v_op, 1)
                        dve.wait_ge(v_op, base + 1)
                        nc.vector.tensor_copy(v_s[0][:, :], vm[:, :]).then_inc(v_op, 1)
                        dve.wait_ge(v_op, base + 2)
                        tt(v_s[1][:, :], vm[:, :], v_s[0][:, :], ALU.subtract).then_inc(v_op, 1)
                    if s in (14, 15) and has_mid(c):
                        for ot in (2 * (s - 14), 2 * (s - 14) + 1):
                            dve.wait_ge(l2_mm, KT * (c - 1) + 2 * (s - 14) + 2)
                            stt(tile(x3, ot), tile(x2, ot), 2.0, p_m[ot // 2][:, (ot % 2) * C:(ot % 2 + 1) * C],
                                ALU.mult, ALU.add).then_inc(x3_done, 1)

            iterations(dve, body)


_OUT = "out_dram"


def kernel(**inputs):
    import numpy as np
    import concourse.bacc as bacc
    from concourse.bass_utils import run_bass_kernel_spmd

    a = {k: np.asarray(v) for k, v in inputs.items()}
    f32 = np.float32

    def tiles(w):
        return w.reshape(w.shape[0] // P, P, -1).transpose(1, 0, 2).reshape(P, -1)

    def column(v):
        return v.reshape(-1, P).T

    xt = a["x"].reshape(B, NCH, S, KT, P).transpose(1, 4, 3, 2, 0).reshape(NCH, P, KT * C)
    xt = np.concatenate([xt, np.zeros((1, P, KT * C), f32)])

    gates = [3, 1, 0, 2]

    def by_gate(w):
        return np.concatenate([w[..., g * D:(g + 1) * D] for g in gates], axis=-1)

    small = np.zeros((P, NSMALL), f32)

    def put(name, v, rows=slice(0, P)):
        small[rows, SMALL[name]] = v

    cond = a["cond_1024"]
    put("cond", tiles(cond.T))
    put("b0", column(by_gate(a["L0_cond_b"])))
    put("conv_b", column(a["L1_cond_conv_b"]))
    put("bo", column(a["L1_cond_bo"]))
    put("b3", column(a["L3_cond_b"]))
    put("b1", column(a["L2_cond_b1"]))
    put("ln_g", column(a["L2_cond_ln_g"]))
    put("ln_b", column(a["L2_cond_ln_b"]))
    put("b2", a["L2_cond_b2"].reshape(2 * KT, P, R).transpose(1, 0, 2).reshape(P, -1))
    put("alpha", np.repeat(column(a["L3_cond_alpha"]), B, axis=1))
    put("bp", a["L1_cond_bp"].reshape(P, 1))
    put("bs", a["L1_cond_bs"].reshape(N, 1), slice(0, N))
    put("a_dt", np.stack([a["L1_cond_A_log"], a["L1_cond_dt_log"]], axis=1), slice(0, N))
    put("mask", np.tile(np.repeat(np.eye(B, dtype=f32), R, axis=0), (1, S)))
    put("ident", np.eye(P, dtype=f32))

    pieces = np.zeros((N_PIECES, P, PIECE), f32)
    for n, w in ((0, a["L0_cond_Wh"]), (2, a["L0_cond_Wx"])):
        t = tiles(by_gate(w))
        pieces[n], pieces[n + 1] = t[:, :PIECE], t[:, PIECE:]
    w3 = a["L3_cond_W"]
    pieces[4] = np.concatenate([tiles(a["L2_cond_base_layer"]), tiles(w3[:, D:].T)], axis=1)
    ws = a["L1_cond_Ws"]
    pieces[5, :, :KT * D + 2 * D] = np.concatenate(
        [tiles(w3[:, :D].T), tiles(a["L1_cond_Wp"]), tiles(np.concatenate([ws, ws], axis=1))], axis=1)
    pieces[5, :N, KT * D + 2 * D:KT * D + 3 * D] = a["L1_cond_Wo"]
    pieces[6, :, :KT * D] = tiles(a["L2_cond_w1"])
    w2 = a["L2_cond_w2"].reshape(KT, P, 2 * KT, P, R).transpose(2, 1, 0, 4, 3)
    pieces[7:] = w2.reshape(2 * KT, P, PIECE)

    arrays = {"xT_dram": xt, "cond_dram": np.ascontiguousarray(cond), "small_dram": small, "pieces_dram": pieces}
    nc = bacc.Bacc("TRN2", target_bir_lowering=False, num_devices=1)
    f = mybir.dt.float32
    args = [nc.dram_tensor(k, v.shape, f, kind="ExternalInput").ap() for k, v in arrays.items()]
    out = nc.dram_tensor(_OUT, (NCH, P, KT * C), f, kind="ExternalOutput").ap()
    cond_resid_kernel(nc, *args, out)
    r = run_bass_kernel_spmd(nc, [arrays], core_ids=[0])
    got = np.asarray(r.results[0][_OUT]).reshape(NCH, P, KT, S, B)
    return np.ascontiguousarray(got.transpose(4, 0, 3, 2, 1).reshape(B, T, D))
```

```python
import concourse.bass as bass
from concourse import mybir
from contextlib import ExitStack

B = 16
T = 512
D = 512
P = 128
KT = D // P
S = 16
C = S * B
NCH = T // S
NG = 4 * D // P
NGIF = 3 * D // P
GIF = NGIF * B
W1 = KT * B
N = 64
TAPS = 16
R = 8
LAG = 5
EPS = 1e-5
PIECE = 4096
HALO = (TAPS - 1) * B

SMALL = {}
_at = 0
for _name, _n in (("cond", W1), ("b0", NG), ("conv_b", KT), ("bo", KT), ("b3", KT), ("b1", KT), ("ln_g", KT),
                  ("ln_b", KT), ("b2", 2 * KT * R), ("alpha", W1), ("bp", 1), ("bs", 1), ("a_dt", 2),
                  ("mask", C), ("ident", P)):
    SMALL[_name] = slice(_at, _at + _n)
    _at += _n
NSMALL = _at

DVE_VAR, DVE_NORM = 3, 5
DVE_AE = DVE_NORM + KT
DVE_LORA = 26
SETUP_DVE = DVE_LORA + 3 * KT + KT + 2
PE_HIDDEN = 2
K_DVE = 2
CONV_OPS = TAPS * K_DVE
CONV_PRODS = TAPS * (KT - K_DVE)
CONV_ADDS = (TAPS - 1) * (KT - K_DVE)
PRODS_PER = 4
RING = 2
CONV_PER = 4
SCAN_OPS = 9
XW_FIRST = 0
XW_COUNT = {0: 2, 1: 1, 2: 1, 3: 1, 4: 1, 5: 1, 6: 2, 7: 2, 8: 1, 9: 1, 10: 1, 11: 1, 12: 1}
X_SPLIT_AT = 13
XW_AT, _at = [], 0
for _s in range(S):
    XW_AT.append(range(_at, _at + XW_COUNT.get(_s, 0)))
    _at += XW_COUNT.get(_s, 0)
assert _at == NG


def lora_read(t):
    return DVE_LORA + (3 * t if t < KT else 2 * KT + t) + 1


N_PIECES = 7 + 2 * KT


def cond_resid_kernel(nc, xT, cond_row, small, pieces, outT):
    f32 = mybir.dt.float32
    bf16 = mybir.dt.bfloat16
    ALU = mybir.AluOpType
    ACT = mybir.ActivationFunctionType

    ctx = ExitStack()
    with ctx:
        def sb(name, cols, dt=f32, parts=P):
            return ctx.enter_context(nc.sbuf_tensor(name, [parts, cols], dt))

        def sem(name):
            return ctx.enter_context(nc.semaphore(name))

        wh = [sb(f"wh_{p}", KT * 4 * D, bf16) for p in ("hi", "lo")]
        wx = [sb(f"wx_{p}", KT * 4 * D, bf16) for p in ("hi", "lo")]
        m1 = [sb(f"base_wz_{p}", 2 * KT * D, bf16) for p in ("hi", "lo")]
        m2 = [sb(f"wg_wp_ws_wo_{p}", PIECE, bf16) for p in ("hi", "lo")]
        lra = [sb(f"lora_a_{p}", KT * P, bf16) for p in ("hi", "lo")]
        lrb = [sb(f"lora_b_{p}", D, bf16) for p in ("hi", "lo")]

        def whs(p, kt, ft):
            return wh[p][:, (kt * NG + ft) * P:(kt * NG + ft + 1) * P]

        def wxs(p, kt, ft):
            return wx[p][:, (kt * NG + ft) * P:(kt * NG + ft + 1) * P]

        def bases(p, kt, ot):
            return m1[p][:, kt * D + ot * P:kt * D + (ot + 1) * P]

        def wzs(p, kt, ot):
            return m1[p][:, (KT + kt) * D + ot * P:(KT + kt) * D + (ot + 1) * P]

        def wgs(p, kt, ot):
            return m2[p][:, kt * D + ot * P:kt * D + (ot + 1) * P]

        def wps(p, kt):
            return m2[p][:, KT * D + kt * P:KT * D + (kt + 1) * P]

        def wss(p, kt):
            return m2[p][:, KT * D + D + kt * P:KT * D + D + (kt + 1) * P]

        def wos(p, ot):
            return m2[p][0:N, KT * D + 2 * D + ot * P:KT * D + 2 * D + (ot + 1) * P]

        sp = sb("small_params", NSMALL)

        def par(name, k=None):
            a = SMALL[name]
            return sp[:, a] if k is None else sp[:, a.start + k:a.start + k + 1]

        leak = sb("leak", W1)
        ssm = sb("ssm_params", 8, parts=N)
        decay_t = sb("decay_tile", C, parts=N)

        xw = sb("xw", 2 * S * NG * B)
        x_in = sb("x_in", KT * C)
        x_s = [sb(f"x_{p}", KT * C, bf16) for p in ("hi", "lo")]
        x_res = sb("x_res", KT * C)
        x1 = sb("x1", KT * C)
        win = sb("win", KT * (HALO + C))
        conv = sb("conv", KT * C)
        conv_s = [sb(f"conv_{p}", KT * C, bf16) for p in ("hi", "lo")]
        win_s = conv_s
        x2, x2_s = conv, conv_s
        x3 = sb("x3", KT * C)
        x3_s = [sb(f"x3_{p}", KT * C, bf16) for p in ("hi", "lo")]
        zw = sb("zw", KT * C)
        z_c = sb("z_cur", S * W1)
        zw_c = sb("zw_cur", S * W1)
        outb = sb("outb", KT * C)
        prod = sb("conv_products", RING * C)
        gsum = sb("gate_sums", NG * B)
        fi = sb("sig_f_i", 2 * W1)
        cg = sb("c_and_g", 2 * W1)
        fcig = sb("fc_ig", 2 * W1)
        so = sb("sig_o", W1)
        tc = sb("tanh_c", W1)
        h0 = sb("h0", W1)
        h0_s = sb("h0_split", 2 * W1, bf16)
        s3 = sb("l3_sums", W1)
        gate3 = sb("l3_gate", W1)
        gz = sb("l3_gz", W1)
        hl = sb("l3_h_leak", W1)
        pre3 = sb("l3_pre", W1)
        h3 = sb("l3_h", W1)
        h3_s = sb("l3_h_split", 2 * W1, bf16)
        spa = sb("sp_terms", C, parts=N)
        spe = spl = spa
        spr = sb("sp_relu", C, parts=N)
        bt = bu = spr
        ct = sb("c_t", C, parts=N)
        vbt = sb("v_bt", C, parts=N)
        state = sb("state", C, parts=N)
        y = vbt
        y_s = [sb(f"y_{p}", C, bf16, parts=N) for p in ("hi", "lo")]
        vm = prod[:, 0:C]
        v_s = [sb(f"lora_v_{p}", C, bf16) for p in ("hi", "lo")]
        crow = outb[0:B, 0:D]
        stats = sb("ln_stats", 16, parts=B)
        ae = x1
        hid = x2
        lrt = x3

        def pb(name):
            return ctx.enter_context(nc.psum_tensor(name, [P, 512], f32))

        p_gif, p_o, p_l3, p_x0, p_x1, p_m0, p_m1, p_p = (
            pb(n) for n in ("p_gif", "p_o", "p_l3", "p_x0", "p_x1", "p_m0", "p_m1", "p_proj"))
        p_x = [p_x0, p_x1]
        p_m = [p_m0, p_m1]

        small_in, piece_in = sem("small_in"), [sem("piece_in_even"), sem("piece_in_odd")]
        piece_split = sem("piece_split")
        x_loaded, res_loaded, out_stored = sem("x_loaded"), sem("res_loaded"), sem("out_stored")
        setup_dve, setup_act, setup_pe = sem("setup_dve"), sem("setup_act"), sem("setup_pe")
        x_split_hi, x_split_lo = sem("x_split_hi"), sem("x_split_lo")
        xw_mm, xw_done = sem("xw_mm"), sem("xw_done")
        gif_mm, o_mm = sem("gif_mm"), sem("o_mm")
        gif_part, gif_sum, o_part, o_sum = sem("gif_part"), sem("gif_sum"), sem("o_part"), sem("o_sum")
        g_tanh, fi_sig, o_sig, c_tanh = sem("g_tanh"), sem("fi_sig"), sem("o_sig"), sem("c_tanh")
        fcig_done, c_new, h0_f32, h0_split, x1_done = (sem(n) for n in ("fcig_done", "c_new", "h0_f32", "h0_split", "x1_done"))
        win_moved, win_hi, win_lo, u_mm, conv_op, conv_hi, conv_lo, proj_mm = (
            sem(n) for n in ("win_moved", "win_hi", "win_lo", "u_mm", "conv_op", "conv_hi", "conv_lo", "proj_mm"))
        conv_prod, conv_add = sem("conv_prod"), sem("conv_add")
        sp_abs, c_done, sp_exp, sp_log, scan_op, wo_mm, x2_done, x2_hi, x2_lo = (
            sem(n) for n in ("sp_abs_done", "c_done", "sp_exp_done", "sp_log_done", "scan_op", "wo_mm", "x2_done",
                             "x2_hi_done", "x2_lo_done"))
        v_mm, v_op, l2_mm, x3_done, x3_hi, x3_lo, zw_mm, zw_done, z_moved = (
            sem(n) for n in ("v_mm", "v_op", "l2_mm", "x3_done", "x3_hi_done", "x3_lo_done", "zw_mm", "zw_done", "z_moved"))
        l3_mm, s3_part, s3_sum, l3_gate, l3_gz, l3_pre, l3_h, l3_split, l3_leak, l3_out = (
            sem(n) for n in ("l3_mm", "s3_part", "s3_sum", "l3_gate_done", "l3_gz_done", "l3_pre_done", "l3_h_done",
                             "l3_split", "l3_leak_done", "l3_out_done"))

        def kb(t, lo, n=W1):
            return t[:, lo:lo + n].rearrange("p (k b) -> p k b", b=B)

        def step_cols(t, s):
            return t[:, :].rearrange("p (k c) -> p k c", k=KT)[:, :, s * B:(s + 1) * B]

        def tile(t, k):
            return t[:, k * C:(k + 1) * C]

        def xw_slots(p):
            return xw[:, bass.ds(p * (S * NG * B), S * NG * B)].rearrange("p (t g) -> p t g", t=S)

        def xw_step(p, s):
            return xw[:, bass.ds(p * (S * NG * B) + s * NG * B, NG * B)].rearrange("p (g b) -> p g b", b=B)

        win_v = win[:, :].rearrange("p (k c) -> p k c", k=KT)
        x1_v = x1[:, :].rearrange("p (k c) -> p k c", k=KT)
        h0_v = h0_s[:, :].rearrange("p (k q b) -> p k q b", q=2, b=B)
        h3_v = h3_s[:, :].rearrange("p (k q b) -> p k q b", q=2, b=B)

        block = ctx.enter_context(nc.Block())

        def has_l0(c):
            return not isinstance(c, int) or c < NCH

        def has_mid(c):
            return not isinstance(c, int) or 1 <= c <= NCH

        def has_z(c):
            return not isinstance(c, int) or 2 <= c <= NCH + 1

        def has_l3(c, s):
            return not isinstance(c, int) or 0 <= S * (c - 2) + s - LAG < T

        def iterations(engine, body):
            for c in (0, 1, 2):
                body(c)
            with engine.Fori(3, NCH) as c:
                body(c)
            for c in (NCH, NCH + 1, NCH + 2):
                body(c)

        @block.sync
        def _(sync):
            sync.dma_start(sp[:, :], small).then_inc(small_in, 16)
            sync.dma_start(crow, cond_row).then_inc(small_in, 16)
            sync.dma_start(x_in[:, :], xT[0, :, :]).then_inc(x_loaded, 16)
            for n in range(N_PIECES):
                if 2 <= n < 8:
                    sync.wait_ge(piece_split, n - 1)
                elif n >= 8:
                    sync.wait_ge(setup_pe, PE_HIDDEN + n - 8)
                sync.dma_start(xw[:, (n % 2) * PIECE:(n % 2 + 1) * PIECE], pieces[n, :, :]).then_inc(piece_in[n % 2], 16)

            sync.wait_ge(x_split_hi, 1)
            sync.wait_ge(x_split_lo, 1)
            sync.dma_start(x_in[:, :], xT[1, :, :]).then_inc(x_loaded, 16)

            def body(c):
                if has_l0(c):
                    sync.wait_ge(x_split_hi, c + 2)
                    sync.wait_ge(x_split_lo, c + 2)
                    sync.dma_start(x_in[:, :], xT[c + 2, :, :]).then_inc(x_loaded, 16)
                    if not (isinstance(c, int) and c == 0):
                        sync.wait_ge(x1_done, S * c)
                    sync.dma_start(x_res[:, :], xT[c, :, :]).then_inc(res_loaded, 16)
                if not isinstance(c, int) or c >= 3:
                    sync.wait_ge(l3_out, S * (c - 2))
                    sync.dma_start(outT[c - 3, :, :], outb[:, :]).then_inc(out_stored, 16)

            iterations(sync, body)
            sync.wait_ge(out_stored, 16 * NCH)
            sync.wait_ge(x_loaded, 16 * (NCH + 2))

        @block.gpsimd
        def _(pool):
            def low(dst, src, hi, done, ready, n):
                pool.wait_ge(ready, n)
                nc.gpsimd.tensor_tensor(dst, src, hi, ALU.subtract).then_inc(done, 1)

            def conv_adds(c, taps):
                for n in taps:
                    j, k = divmod(n, KT - K_DVE)
                    if j == 0:
                        continue
                    a = n - (KT - K_DVE)
                    pool.wait_ge(conv_prod, CONV_PRODS * (c - 1) + n + 1)
                    if j > 1:
                        pool.wait_ge(conv_add, CONV_ADDS * (c - 1) + a - (KT - K_DVE) + 1)
                    t = tile(conv, K_DVE + k)
                    nc.gpsimd.tensor_tensor(t, t, prod[:, (n % RING) * C:(n % RING + 1) * C], ALU.add).then_inc(conv_add, 1)

            def splits(c, s):
                if s == X_SPLIT_AT and has_l0(c):
                    low(x_s[1][:, :], x_in[:, :], x_s[0][:, :], x_split_lo, x_split_hi, c + 3)
                if s == 0 and has_z(c):
                    low(x3_s[1][:, :], x3[:, :], x3_s[0][:, :], x3_lo, x3_hi, c - 1)
                if s == 1 and has_mid(c):
                    pool.wait_ge(win_hi, c)
                    nc.gpsimd.tensor_tensor(win_s[1][:, :].rearrange("p (k c) -> p k c", k=KT), win_v[:, :, HALO:],
                                            win_s[0][:, :].rearrange("p (k c) -> p k c", k=KT),
                                            ALU.subtract).then_inc(win_lo, 1)
                if s == 8 and has_mid(c):
                    low(conv_s[1][:, :], conv[:, :], conv_s[0][:, :], conv_lo, conv_hi, c)
                if s == 12 and has_mid(c):
                    low(x2_s[1][:, :], x2[:, :], x2_s[0][:, :], x2_lo, x2_hi, c)
                if has_mid(c):
                    conv_adds(c, range(PRODS_PER * s, min(PRODS_PER * (s + 1), CONV_PRODS)))

            low(x_s[1][:, :], x_in[:, :], x_s[0][:, :], x_split_lo, x_split_hi, 1)
            low(x_s[1][:, :], x_in[:, :], x_s[0][:, :], x_split_lo, x_split_hi, 2)

            def body(c):
                m = c - 1
                for s in range(S):
                    g3 = S * (c - 2) + s - LAG
                    if not has_l3(c, s):
                        splits(c, s)
                    if has_l3(c, s):
                        if not (isinstance(c, int) and c == 2 and s == LAG):
                            pool.wait_ge(l3_h, g3)
                            pool.wait_ge(l3_pre, g3)
                        else:
                            pool.wait_ge(setup_dve, SETUP_DVE)
                        nc.gpsimd.tensor_tensor(hl[:, :], h3[:, :], leak[:, :], ALU.mult).then_inc(l3_leak, 1)
                        splits(c, s)
                        if s == LAG and not (isinstance(c, int) and c == 2):
                            pool.wait_ge(out_stored, 16 * (c - 2))
                        pool.wait_ge(l3_h, g3 + 1)
                        t = (s - LAG) % S
                        nc.gpsimd.tensor_tensor(step_cols(outb, t), kb(z_c, t * W1), kb(h3, 0), ALU.add).then_inc(l3_out, 1)

            iterations(pool, body)

        SETUP_ACT = {}

        @block.scalar
        def _(act):
            done = [0]

            def setup(name, ins):
                ins.then_inc(setup_act, 1)
                done[0] += 1
                SETUP_ACT[name] = done[0]

            act.wait_ge(small_in, 32)
            setup("abs", nc.scalar.activation(ssm[:, 3:5], par("a_dt")[0:N, :], ACT.Abs))
            act.wait_ge(setup_act, 1)
            setup("exp", nc.scalar.activation(ssm[:, 5:7], ssm[:, 3:5], ACT.Exp, scale=-1.0))
            act.wait_ge(setup_act, 2)
            setup("log", nc.scalar.activation(ssm[:, 3:5], ssm[:, 5:7], ACT.Ln, bias=1.0))
            act.wait_ge(setup_dve, DVE_VAR)
            setup("std", nc.scalar.activation(stats[:, 9:10], stats[:, 8:9], ACT.Sqrt))
            act.wait_ge(setup_pe, 2)
            for it in range(KT):
                setup("gelu", nc.scalar.activation(hid[:, it * B:(it + 1) * B], p_p[:, 64 + it * B:64 + (it + 1) * B],
                                                   ACT.Gelu, bias=par("b1", it)))

            def high(dst, src, done, ready, n):
                act.wait_ge(ready, n)
                nc.scalar.activation(dst, src, ACT.Copy).then_inc(done, 1)

            def xw_out(q, par_, ft):
                act.wait_ge(xw_mm, NG * q + ft + 1)
                out = xw_slots(par_)[:, :, ft * B:(ft + 1) * B]
                nc.scalar.activation(out, p_x[ft % 2][:, 0:C].rearrange("p (t b) -> p t b", b=B), ACT.Identity,
                                     bias=par("b0", ft)).then_inc(xw_done, 1)

            high(x_s[0][:, :], x_in[:, :], x_split_hi, x_loaded, 16)
            act.wait_ge(setup_pe, PE_HIDDEN + 2 * KT)
            for ft in range(NG):
                xw_out(0, 0, ft)
            high(x_s[0][:, :], x_in[:, :], x_split_hi, x_loaded, 32)

            def conv_products(c, taps):
                for n in taps:
                    j, k = divmod(n, KT - K_DVE)
                    k += K_DVE
                    src = win[:, k * (HALO + C) + j * B:k * (HALO + C) + j * B + C]
                    w = sp[:, SMALL["cond"].start + k * B + j:SMALL["cond"].start + k * B + j + 1]
                    if j == 0:
                        ins = nc.scalar.activation(tile(conv, k), src, ACT.Identity, scale=w, bias=par("conv_b", k))
                    else:
                        if n - RING >= KT - K_DVE:
                            act.wait_ge(conv_add, CONV_ADDS * (c - 1) + n - RING - (KT - K_DVE) + 1)
                        ins = nc.scalar.activation(prod[:, (n % RING) * C:(n % RING + 1) * C], src, ACT.Identity,
                                                   scale=w)
                    ins.then_inc(conv_prod, 1)

            def body(c):
                for s in range(S):
                    g = S * c + s
                    g3 = S * (c - 2) + s - LAG
                    prods = range(PRODS_PER * s, min(PRODS_PER * (s + 1), CONV_PRODS)) if has_mid(c) else ()
                    if s == 0 and has_mid(c):
                        act.wait_ge(win_moved, 2 * c)
                    if s == X_SPLIT_AT and has_l0(c):
                        act.wait_ge(xw_mm, NG * (c + 2))
                        high(x_s[0][:, :], x_in[:, :], x_split_hi, x_loaded, 16 * (c + 3))
                    if s == 0 and has_z(c):
                        high(x3_s[0][:, :], x3[:, :], x3_hi, x3_done, KT * (c - 1))
                    if has_l3(c, s):
                        act.wait_ge(s3_sum, g3 + 1)
                        nc.scalar.activation(gate3[:, :], s3[:, :], ACT.Sigmoid).then_inc(l3_gate, 1)
                        act.wait_ge(l3_pre, g3 + 1)
                        if not (isinstance(c, int) and c == 2 and s == LAG):
                            act.wait_ge(l3_split, 2 * g3 + 2)
                            act.wait_ge(l3_out, g3)
                        act.wait_ge(l3_leak, g3 + 1)
                        nc.scalar.activation(h3[:, :], pre3[:, :], ACT.Tanh).then_inc(l3_h, 1)
                    conv_products(c, prods[:2])
                    if has_l0(c):
                        act.wait_ge(gif_sum, g + 1)
                        nc.scalar.activation(fi[:, :], gsum[:, W1:3 * W1], ACT.Sigmoid).then_inc(fi_sig, 1)
                        nc.scalar.activation(cg[:, W1:2 * W1], gsum[:, 0:W1], ACT.Tanh).then_inc(g_tanh, 1)
                        act.wait_ge(o_sum, g + 1)
                        nc.scalar.activation(so[:, :], gsum[:, 3 * W1:4 * W1], ACT.Sigmoid).then_inc(o_sig, 1)
                        act.wait_ge(c_new, g + 1)
                        nc.scalar.activation(tc[:, :], cg[:, 0:W1], ACT.Tanh).then_inc(c_tanh, 1)
                    if s == 0 and has_mid(c):
                        act.wait_ge(win_moved, 2 * c)
                        nc.scalar.activation(win_s[0][:, :].rearrange("p (k c) -> p k c", k=KT), win_v[:, :, HALO:],
                                             ACT.Copy).then_inc(win_hi, 1)
                    conv_products(c, prods[2:])
                    if s == 7 and has_mid(c):
                        act.wait_ge(conv_add, CONV_ADDS * c)
                        high(conv_s[0][:, :], conv[:, :], conv_hi, conv_op, CONV_OPS * c)
                    if s == 9 and has_mid(c):
                        act.wait_ge(proj_mm, c)
                        nc.scalar.activation(spa[:, :], p_p[0:N, 0:C], ACT.Abs, bias=par("bp")[0:N, :]).then_inc(sp_abs, 1)
                        nc.scalar.activation(ct[:, :], p_p[N:P, 0:C], ACT.Tanh, bias=par("bp")[N:P, :]).then_inc(c_done, 1)
                        nc.scalar.preload_act_table_set("natural_log_exp_and_others")
                        act.wait_ge(sp_abs, c)
                        nc.scalar.activation(spe[:, :], spa[:, :], ACT.Exp, scale=-1.0).then_inc(sp_exp, 1)
                        act.wait_ge(sp_exp, c)
                        nc.scalar.activation(spl[:, :], spe[:, :], ACT.Ln, bias=1.0).then_inc(sp_log, 1)
                    if s == 11 and has_mid(c):
                        high(x2_s[0][:, :], x2[:, :], x2_hi, x2_done, KT * c)
                    if s in (2, 4) and has_z(c):
                        for ot in (s - 2, s - 1):
                            act.wait_ge(zw_mm, KT * (c - 2) + s)
                            nc.scalar.activation(tile(zw, ot), p_m[ot // 2][:, (ot % 2) * C:(ot % 2 + 1) * C], ACT.Identity,
                                                 bias=par("b3", ot)).then_inc(zw_done, 1)
                    if has_l0(c):
                        for ft in XW_AT[s]:
                            xw_out(c + 1, (c + 1) % 2, ft)

            iterations(act, body)

        @block.tensor
        def _(pe):
            mm = nc.tensor.matmul

            def three(out, ws, xs, kts, first, last):
                todo = [(k, a, b) for k in kts for a, b in ((0, 0), (0, 1), (1, 0))]
                ins = None
                for n, (k, a, b) in enumerate(todo):
                    ins = mm(out, ws(a, k), xs(b, k), start=first and n == 0, stop=last and n == len(todo) - 1)
                return ins

            pe.wait_ge(setup_dve, DVE_NORM)
            for k in range(KT):
                ins = nc.tensor.transpose(p_p[:, k * B:(k + 1) * B], outb[0:B, k * P:(k + 1) * P], par("ident")[0:B, 0:B])
            ins.then_inc(setup_pe, 1)
            pe.wait_ge(piece_in[0], 16 * 4)
            pe.wait_ge(setup_dve, DVE_AE)
            for it in range(KT):
                for k in range(KT):
                    ins = mm(p_p[:, 64 + it * B:64 + (it + 1) * B], xw[:, k * D + it * P:k * D + (it + 1) * P],
                             ae[:, k * B:(k + 1) * B], start=k == 0, stop=k == KT - 1)
            ins.then_inc(setup_pe, 1)
            pe.wait_ge(setup_act, SETUP_ACT["gelu"])
            for t in range(2 * KT):
                n = 7 + t
                pe.wait_ge(piece_in[n % 2], 16 * (n // 2 + 1))
                if t >= 2:
                    pe.wait_ge(setup_dve, lora_read(t - 2))
                for r in range(R):
                    for k in range(KT):
                        ins = mm(p_m[t % 2][:, r * B:(r + 1) * B],
                                 xw[:, (n % 2) * PIECE + (k * R + r) * P:(n % 2) * PIECE + (k * R + r + 1) * P],
                                 hid[:, k * B:(k + 1) * B], start=k == 0, stop=k == KT - 1)
                ins.then_inc(setup_pe, 1)
            pe.wait_ge(setup_dve, lora_read(2 * KT - 1))
            for t in range(KT):
                ins = nc.tensor.transpose(p_p[:, t * P:(t + 1) * P], lrt[:, t * P:(t + 1) * P], par("ident"))
            ins.then_inc(setup_pe, 1)

            def xw_products(q, ft):
                if isinstance(q, int) and q == 0 and ft < 2:
                    pass
                else:
                    pe.wait_ge(xw_done, NG * q + ft - 1)
                three(p_x[ft % 2][:, 0:C], lambda a, k: wxs(a, k, ft), lambda b, k: tile(x_s[b], k), range(KT),
                      True, True).then_inc(xw_mm, 1)

            def gate_products(bank, fts, wait_low):
                for n, ft in enumerate(fts):
                    for k in range(KT):
                        mm(bank[:, n * 2 * B:n * 2 * B + B], whs(1, k, ft), h0_s[:, k * 2 * B:k * 2 * B + B],
                           start=n == 0 and k == 0, stop=False, skip_group_check=True)
                if wait_low is not None:
                    pe.wait_ge(h0_split, wait_low)
                for n, ft in enumerate(fts):
                    for k in range(KT):
                        ins = mm(bank[:, n * 2 * B:(n + 1) * 2 * B], whs(0, k, ft), h0_s[:, k * 2 * B:(k + 1) * 2 * B],
                                 start=False, stop=ft == fts[-1] and k == KT - 1, skip_group_check=True)
                return ins

            def lstm_products(c, s):
                g = S * c + s
                pe.wait_ge(h0_split, 2 * g + 1)
                gate_products(p_gif, range(NGIF), 2 * g + 2).then_inc(gif_mm, 1)
                gate_products(p_o, range(NGIF, NG), None).then_inc(o_mm, 1)

            def l3_products(g3):
                pe.wait_ge(l3_split, 2 * g3 + 2)
                for ot in range(KT):
                    for k in range(KT):
                        mm(p_l3[:, ot * 2 * B:(ot + 1) * 2 * B], wgs(0, k, ot), h3_s[:, k * 2 * B:(k + 1) * 2 * B],
                           start=k == 0, stop=False)
                    for k in range(KT):
                        ins = mm(p_l3[:, ot * 2 * B:ot * 2 * B + B], wgs(1, k, ot), h3_s[:, k * 2 * B:k * 2 * B + B],
                                 start=False, stop=k == KT - 1)
                ins.then_inc(l3_mm, 1)

            pe.wait_ge(piece_split, 6)
            pe.wait_ge(setup_dve, SETUP_DVE)
            pe.wait_ge(x_split_hi, 1)
            pe.wait_ge(x_split_lo, 1)
            for ft in range(NG):
                xw_products(0, ft)

            def body(c):
                for s in range(S):
                    if has_l3(c, s):
                        l3_products(S * (c - 2) + s - LAG)
                    if has_l0(c):
                        lstm_products(c, s)
                    if s in (1, 2, 3, 4) and has_z(c):
                        if s == 1:
                            pe.wait_ge(x3_hi, c - 1)
                            pe.wait_ge(x3_lo, c - 1)
                        for ot in (s - 1,):
                            three(p_m[ot // 2][:, (ot % 2) * C:(ot % 2 + 1) * C], lambda a, k: wzs(a, k, ot),
                                  lambda b, k: tile(x3_s[b], k), range(KT), True, True).then_inc(zw_mm, 1)
                    if s == 5 and has_mid(c):
                        pe.wait_ge(win_hi, c)
                        pe.wait_ge(win_lo, c)
                        three(p_p[:, C:2 * C], lambda a, k: wss(a, k), lambda b, k: tile(win_s[b], k), range(KT),
                              True, True).then_inc(u_mm, 1)
                    if s == 9 and has_mid(c):
                        pe.wait_ge(conv_hi, c)
                        pe.wait_ge(conv_lo, c)
                        three(p_p[:, 0:C], lambda a, k: wps(a, k), lambda b, k: tile(conv_s[b], k), range(KT),
                              True, True).then_inc(proj_mm, 1)
                    if s == 11 and has_mid(c):
                        pe.wait_ge(scan_op, SCAN_OPS * c)
                        for ot in range(KT):
                            three(p_m[ot // 2][:, (ot % 2) * C:(ot % 2 + 1) * C], lambda a, k: wos(a, ot),
                                  lambda b, k: y_s[b][:, :], (0,), True, True).then_inc(wo_mm, 1)
                    if s == 13 and has_mid(c):
                        pe.wait_ge(x2_hi, c)
                        pe.wait_ge(x2_lo, c)
                        three(p_p[:, 0:C], lambda a, k: lra[a][:, k * P:(k + 1) * P], lambda b, k: tile(x2_s[b], k),
                              range(KT), True, True).then_inc(v_mm, 1)
                    if s in (14, 15) and has_mid(c):
                        pe.wait_ge(v_op, 3 * c)
                        for ot in (2 * (s - 14), 2 * (s - 14) + 1):
                            out = p_m[ot // 2][:, (ot % 2) * C:(ot % 2 + 1) * C]
                            three(out, lambda a, k: bases(a, k, ot), lambda b, k: tile(x2_s[b], k), range(KT), True, False)
                            three(out, lambda a, k: lrb[a][:, ot * P:(ot + 1) * P], lambda b, k: v_s[b][:, :], (0,),
                                  False, True).then_inc(l2_mm, 1)
                    if has_l0(c) and XW_AT[s]:
                        if s == XW_FIRST:
                            pe.wait_ge(x_split_hi, c + 2)
                            pe.wait_ge(x_split_lo, c + 2)
                        for ft in XW_AT[s]:
                            xw_products(c + 1, ft)

            iterations(pe, body)

        @block.vector
        def _(dve):
            tt, ts, stt = nc.vector.tensor_tensor, nc.vector.tensor_scalar, nc.vector.scalar_tensor_tensor
            n_setup = [0]

            def setup(ins):
                ins.then_inc(setup_dve, 1)
                n_setup[0] += 1

            def settled():
                dve.wait_ge(setup_dve, n_setup[0])

            dve.wait_ge(small_in, 32)
            setup(nc.vector.bn_stats(stats[:, 0:6], crow))
            settled()
            setup(nc.vector.bn_aggr(stats[:, 6:8], stats[:, 0:6]))
            settled()
            setup(ts(stats[:, 8:9], stats[:, 7:8], EPS, None, ALU.add))
            assert n_setup[0] == DVE_VAR
            dve.wait_ge(setup_act, SETUP_ACT["std"])
            setup(nc.vector.reciprocal(stats[:, 10:11], stats[:, 9:10]))
            settled()
            setup(ts(crow, crow, stats[:, 6:7], stats[:, 10:11], ALU.subtract, ALU.mult))
            assert n_setup[0] == DVE_NORM
            dve.wait_ge(setup_pe, 1)
            for k in range(KT):
                setup(ts(ae[:, k * B:(k + 1) * B], p_p[:, k * B:(k + 1) * B], par("ln_g", k), par("ln_b", k),
                         ALU.mult, ALU.add))
            assert n_setup[0] == DVE_AE
            setup(stt(ssm[:, 0:2], par("a_dt")[0:N, :], 0.0, ssm[:, 3:5], ALU.max, ALU.add))
            settled()
            setup(tt(ssm[:, 2:3], ssm[:, 0:1], ssm[:, 1:2], ALU.mult))
            setup(nc.vector.memset(decay_t[:, :], 1.0))
            settled()
            setup(ts(ssm[:, 2:3], ssm[:, 2:3], -1.0, 1.0, ALU.mult, ALU.add))
            setup(nc.vector.memset(decay_t[:, :].rearrange("p (b t) -> p b t", t=S)[:, :, 0], 0.0))
            settled()
            setup(ts(decay_t[:, :], decay_t[:, :], ssm[:, 2:3], None, ALU.mult))
            setup(nc.vector.memset(cg[:, :], 0.0))
            setup(nc.vector.memset(win[:, :], 0.0))
            setup(nc.vector.memset(state[:, :], 0.0))
            setup(ts(leak[:, :], par("alpha"), -1.0, 1.0, ALU.mult, ALU.add))
            setup(nc.vector.tensor_copy(h3[:, :], par("cond")))
            for v, done in ((h0_v, h0_split), (h3_v, l3_split)):
                nc.vector.tensor_copy(v[:, :, 0, :], kb(par("cond"), 0)).then_inc(done, 1)
                dve.wait_ge(done, 1)
                tt(v[:, :, 1, :], kb(par("cond"), 0), v[:, :, 0, :], ALU.subtract).then_inc(done, 1)

            places = [(wh, 0), (wh, PIECE), (wx, 0), (wx, PIECE), (m1, 0), (m2, 0)]
            for n, (dst, at) in enumerate(places):
                src = xw[:, (n % 2) * PIECE:(n % 2 + 1) * PIECE]
                dve.wait_ge(piece_in[n % 2], 16 * (n // 2 + 1))
                setup(nc.vector.tensor_copy(dst[0][:, at:at + PIECE], src))
                settled()
                tt(dst[1][:, at:at + PIECE], src, dst[0][:, at:at + PIECE], ALU.subtract).then_inc(piece_split, 1)
            assert n_setup[0] == DVE_LORA
            for t in range(2 * KT):
                dve.wait_ge(setup_pe, 3 + t)
                if t == KT:
                    settled()
                b2 = sp[:, SMALL["b2"].start + t * R:SMALL["b2"].start + (t + 1) * R]
                out = lrt[:, (t % KT) * P:(t % KT + 1) * P].rearrange("p (b r) -> p r b", r=R)
                setup(tt(out, p_m[t % 2][:, 0:P].rearrange("p (r b) -> p r b", b=B),
                         b2.unsqueeze(2).to_broadcast([P, R, B]), ALU.add))
                settled()
                if t < KT:
                    a = lra[0][:, t * P:(t + 1) * P]
                    setup(nc.vector.tensor_copy(a, lrt[:, t * P:(t + 1) * P]))
                    settled()
                    setup(tt(lra[1][:, t * P:(t + 1) * P], lrt[:, t * P:(t + 1) * P], a, ALU.subtract))
            dve.wait_ge(setup_pe, 3 + 2 * KT)
            setup(nc.vector.tensor_copy(lrb[0][:, :], p_p[:, :]))
            settled()
            setup(tt(lrb[1][:, :], p_p[:, :], lrb[0][:, :], ALU.subtract))
            assert n_setup[0] == SETUP_DVE, n_setup[0]
            settled()

            def conv_tap(c, n):
                j, k = divmod(n, K_DVE)
                base = CONV_OPS * (c - 1)
                src = win[:, k * (HALO + C) + j * B:k * (HALO + C) + j * B + C]
                w = sp[:, SMALL["cond"].start + k * B + j:SMALL["cond"].start + k * B + j + 1]
                if j == 0:
                    ins = ts(tile(conv, k), src, w, par("conv_b", k), ALU.mult, ALU.add)
                else:
                    dve.wait_ge(conv_op, base + n - K_DVE + 1)
                    ins = stt(tile(conv, k), src, w, tile(conv, k), ALU.mult, ALU.add)
                ins.then_inc(conv_op, 1)

            def lstm_step(c, s, taps):
                g = S * c + s
                p = c % 2
                dve.wait_ge(gif_mm, g + 1)
                if s == 0:
                    dve.wait_ge(xw_done, NG * (c + 1))
                    dve.wait_ge(res_loaded, 16 * (c + 1))
                lo = p_gif[:, 0:2 * GIF].rearrange("p (k q b) -> p k q b", q=2, b=B)
                tt(kb(gsum, 0, GIF), lo[:, :, 1, :], xw_step(p, s)[:, 0:NGIF, :], ALU.add).then_inc(gif_part, 1)
                dve.wait_ge(gif_part, g + 1)
                tt(kb(gsum, 0, GIF), lo[:, :, 0, :], kb(gsum, 0, GIF), ALU.add).then_inc(gif_sum, 1)
                dve.wait_ge(o_mm, g + 1)
                lo = p_o[:, 0:2 * W1].rearrange("p (k q b) -> p k q b", q=2, b=B)
                tt(kb(gsum, GIF), lo[:, :, 1, :], xw_step(p, s)[:, NGIF:NG, :], ALU.add).then_inc(o_part, 1)
                dve.wait_ge(o_part, g + 1)
                tt(kb(gsum, GIF), lo[:, :, 0, :], kb(gsum, GIF), ALU.add).then_inc(o_sum, 1)
                dve.wait_ge(g_tanh, g + 1)
                dve.wait_ge(fi_sig, g + 1)
                tt(fcig[:, :], fi[:, :], cg[:, :], ALU.mult).then_inc(fcig_done, 1)
                dve.wait_ge(fcig_done, g + 1)
                tt(cg[:, 0:W1], fcig[:, 0:W1], fcig[:, W1:2 * W1], ALU.add).then_inc(c_new, 1)
                for n in taps:
                    conv_tap(c, n)
                dve.wait_ge(o_sig, g + 1)
                dve.wait_ge(c_tanh, g + 1)
                tt(h0_v[:, :, 0, :], kb(so, 0), kb(tc, 0), ALU.mult).then_inc(h0_split, 1)
                tt(h0[:, :], so[:, :], tc[:, :], ALU.mult).then_inc(h0_f32, 1)
                dve.wait_ge(h0_f32, g + 1)
                dve.wait_ge(h0_split, 2 * g + 3)
                tt(h0_v[:, :, 1, :], kb(h0, 0), h0_v[:, :, 0, :], ALU.subtract).then_inc(h0_split, 1)
                tt(step_cols(x1, s), step_cols(x_res, s), kb(h0, 0), ALU.add).then_inc(x1_done, 1)

            def body(c):
                m = c - 1
                for s in range(S):
                    g3 = S * (c - 2) + s - LAG
                    if s == 0 and has_mid(c):
                        dve.wait_ge(x1_done, S * c)
                        if not (isinstance(c, int) and c == 1):
                            dve.wait_ge(win_lo, c - 1)
                            dve.wait_ge(conv_op, CONV_OPS * (c - 1))
                            dve.wait_ge(conv_add, CONV_ADDS * (c - 1))
                        nc.vector.tensor_copy(win_v[:, :, 0:HALO], win_v[:, :, C:C + HALO]).then_inc(win_moved, 1)
                        dve.wait_ge(win_moved, 2 * c - 1)
                        nc.vector.tensor_copy(win_v[:, :, HALO:HALO + C], x1_v).then_inc(win_moved, 1)
                    if s == LAG and has_z(c):
                        if not (isinstance(c, int) and c == 2):
                            dve.wait_ge(l3_out, S * (c - 2))
                        nc.vector.tensor_copy(z_c[:, :].rearrange("p (t k b) -> p k t b", k=KT, b=B),
                                              x3[:, :].rearrange("p (k t b) -> p k t b", k=KT, b=B)).then_inc(z_moved, 1)
                        dve.wait_ge(zw_done, KT * (c - 1))
                        nc.vector.tensor_copy(zw_c[:, :].rearrange("p (t k b) -> p k t b", k=KT, b=B),
                                              zw[:, :].rearrange("p (k t b) -> p k t b", k=KT, b=B)).then_inc(z_moved, 1)
                        dve.wait_ge(z_moved, 2 * (c - 1))
                    if s == 0 and has_mid(c):
                        dve.wait_ge(win_moved, 2 * c)
                    conv_now = list(range(CONV_PER * s, min(CONV_PER * (s + 1), CONV_OPS))) if has_mid(c) else []
                    if has_l3(c, s):
                        t = (s - LAG) % S
                        for n in conv_now[:1]:
                            conv_tap(c, n)
                        conv_now = conv_now[1:]
                        dve.wait_ge(l3_mm, g3 + 1)
                        v = p_l3[:, 0:2 * W1].rearrange("p (k q b) -> p k q b", q=2, b=B)
                        tt(kb(s3, 0), v[:, :, 1, :], kb(zw_c, t * W1), ALU.add).then_inc(s3_part, 1)
                        dve.wait_ge(s3_part, g3 + 1)
                        tt(kb(s3, 0), v[:, :, 0, :], kb(s3, 0), ALU.add).then_inc(s3_sum, 1)
                        for n in conv_now[:1]:
                            conv_tap(c, n)
                        dve.wait_ge(l3_gate, g3 + 1)
                        tt(gz[:, :], gate3[:, :], z_c[:, t * W1:(t + 1) * W1], ALU.mult).then_inc(l3_gz, 1)
                        dve.wait_ge(l3_gz, g3 + 1)
                        dve.wait_ge(l3_leak, g3 + 1)
                        tt(pre3[:, :], gz[:, :], hl[:, :], ALU.add).then_inc(l3_pre, 1)
                        for n in conv_now[1:2]:
                            conv_tap(c, n)
                        dve.wait_ge(l3_h, g3 + 1)
                        nc.vector.tensor_copy(h3_v[:, :, 0, :], kb(h3, 0)).then_inc(l3_split, 1)
                        dve.wait_ge(l3_split, 2 * g3 + 3)
                        tt(h3_v[:, :, 1, :], kb(h3, 0), h3_v[:, :, 0, :], ALU.subtract).then_inc(l3_split, 1)
                        conv_now = conv_now[2:]
                    if has_l0(c):
                        for n in conv_now[:-1]:
                            conv_tap(c, n)
                        lstm_step(c, s, conv_now[-1:])
                    else:
                        for n in conv_now:
                            conv_tap(c, n)
                    if s == 10 and has_mid(c):
                        q = SCAN_OPS * (c - 1)
                        dve.wait_ge(sp_abs, c)
                        dve.wait_ge(c_done, c)
                        dve.wait_ge(u_mm, c)
                        ts(spr[:, :], p_p[0:N, 0:C], par("bp")[0:N, :], 0.0, ALU.add, ALU.max).then_inc(scan_op, 1)
                        dve.wait_ge(scan_op, q + 1)
                        dve.wait_ge(sp_log, c)
                        tt(bt[:, :], spr[:, :], spl[:, :], ALU.add).then_inc(scan_op, 1)
                        dve.wait_ge(scan_op, q + 2)
                        stt(bu[:, :], p_p[0:N, C:2 * C], par("bs")[0:N, :], bt[:, :], ALU.add, ALU.mult).then_inc(scan_op, 1)
                        dve.wait_ge(scan_op, q + 3)
                        ts(vbt[:, :].rearrange("p (b t) -> p t b", t=S), bu[:, :].rearrange("p (t b) -> p t b", b=B),
                           ssm[:, 1:2], None, ALU.mult).then_inc(scan_op, 1)
                        dve.wait_ge(scan_op, q + 4)
                        first = vbt[:, :].rearrange("p (b t) -> p b t", t=S)[:, :, 0]
                        last = state[:, :].rearrange("p (b t) -> p b t", t=S)[:, :, S - 1]
                        stt(first, last, ssm[:, 2:3], first, ALU.mult, ALU.add).then_inc(scan_op, 1)
                        dve.wait_ge(scan_op, q + 5)
                        nc.vector.tensor_tensor_scan(state[:, :], decay_t[:, :], vbt[:, :], 0.0, ALU.mult,
                                                     ALU.add).then_inc(scan_op, 1)
                        dve.wait_ge(scan_op, q + 6)
                        tt(y[:, :].rearrange("p (t b) -> p t b", b=B), state[:, :].rearrange("p (b t) -> p t b", t=S),
                           ct[:, :].rearrange("p (t b) -> p t b", b=B), ALU.mult).then_inc(scan_op, 1)
                        dve.wait_ge(scan_op, q + 7)
                        nc.vector.tensor_copy(y_s[0][:, :], y[:, :]).then_inc(scan_op, 1)
                        dve.wait_ge(scan_op, q + 8)
                        tt(y_s[1][:, :], y[:, :], y_s[0][:, :], ALU.subtract).then_inc(scan_op, 1)
                    if s == 11 and has_mid(c):
                        for ot in range(KT):
                            dve.wait_ge(wo_mm, KT * (c - 1) + KT)
                            win_k = win[:, ot * (HALO + C) + HALO:(ot + 1) * (HALO + C)]
                            stt(tile(x2, ot), p_m[ot // 2][:, (ot % 2) * C:(ot % 2 + 1) * C], par("bo", ot), win_k,
                                ALU.add, ALU.add).then_inc(x2_done, 1)
                    if s == 13 and has_mid(c):
                        dve.wait_ge(v_mm, c)
                        base = 3 * (c - 1)
                        tt(vm, p_p[:, 0:C], par("mask"), ALU.mult).then_inc(v_op, 1)
                        dve.wait_ge(v_op, base + 1)
                        nc.vector.tensor_copy(v_s[0][:, :], vm).then_inc(v_op, 1)
                        dve.wait_ge(v_op, base + 2)
                        tt(v_s[1][:, :], vm, v_s[0][:, :], ALU.subtract).then_inc(v_op, 1)
                    if s in (14, 15) and has_mid(c):
                        for ot in (2 * (s - 14), 2 * (s - 14) + 1):
                            dve.wait_ge(l2_mm, KT * (c - 1) + 2 * (s - 14) + 2)
                            stt(tile(x3, ot), tile(x2, ot), 2.0, p_m[ot // 2][:, (ot % 2) * C:(ot % 2 + 1) * C],
                                ALU.mult, ALU.add).then_inc(x3_done, 1)

            iterations(dve, body)


_OUT = "out_dram"


def kernel(**inputs):
    import numpy as np
    import concourse.bacc as bacc
    from concourse.bass_utils import run_bass_kernel_spmd

    a = {k: np.asarray(v) for k, v in inputs.items()}
    f32 = np.float32

    def tiles(w):
        return w.reshape(w.shape[0] // P, P, -1).transpose(1, 0, 2).reshape(P, -1)

    def column(v):
        return v.reshape(-1, P).T

    xt = a["x"].reshape(B, NCH, S, KT, P).transpose(1, 4, 3, 2, 0).reshape(NCH, P, KT * C)
    xt = np.concatenate([xt, np.zeros((2, P, KT * C), f32)])

    gates = [3, 1, 0, 2]

    def by_gate(w):
        return np.concatenate([w[..., g * D:(g + 1) * D] for g in gates], axis=-1)

    small = np.zeros((P, NSMALL), f32)

    def put(name, v, rows=slice(0, P)):
        small[rows, SMALL[name]] = v

    cond = a["cond_1024"]
    put("cond", tiles(cond.T))
    put("b0", column(by_gate(a["L0_cond_b"])))
    put("conv_b", column(a["L1_cond_conv_b"]))
    put("bo", column(a["L1_cond_bo"]))
    put("b3", column(a["L3_cond_b"]))
    put("b1", column(a["L2_cond_b1"]))
    put("ln_g", column(a["L2_cond_ln_g"]))
    put("ln_b", column(a["L2_cond_ln_b"]))
    put("b2", a["L2_cond_b2"].reshape(2 * KT, P, R).transpose(1, 0, 2).reshape(P, -1))
    put("alpha", np.repeat(column(a["L3_cond_alpha"]), B, axis=1))
    put("bp", a["L1_cond_bp"].reshape(P, 1))
    put("bs", a["L1_cond_bs"].reshape(N, 1), slice(0, N))
    put("a_dt", np.stack([a["L1_cond_A_log"], a["L1_cond_dt_log"]], axis=1), slice(0, N))
    put("mask", np.tile(np.repeat(np.eye(B, dtype=f32), R, axis=0), (1, S)))
    put("ident", np.eye(P, dtype=f32))

    pieces = np.zeros((N_PIECES, P, PIECE), f32)
    for n, w in ((0, a["L0_cond_Wh"]), (2, a["L0_cond_Wx"])):
        t = tiles(by_gate(w))
        pieces[n], pieces[n + 1] = t[:, :PIECE], t[:, PIECE:]
    w3 = a["L3_cond_W"]
    pieces[4] = np.concatenate([tiles(a["L2_cond_base_layer"]), tiles(w3[:, D:].T)], axis=1)
    ws = a["L1_cond_Ws"]
    pieces[5, :, :KT * D + 2 * D] = np.concatenate(
        [tiles(w3[:, :D].T), tiles(a["L1_cond_Wp"]), tiles(np.concatenate([ws, ws], axis=1))], axis=1)
    pieces[5, :N, KT * D + 2 * D:KT * D + 3 * D] = a["L1_cond_Wo"]
    pieces[6, :, :KT * D] = tiles(a["L2_cond_w1"])
    w2 = a["L2_cond_w2"].reshape(KT, P, 2 * KT, P, R).transpose(2, 1, 0, 4, 3)
    pieces[7:] = w2.reshape(2 * KT, P, PIECE)

    arrays = {"xT_dram": xt, "cond_dram": np.ascontiguousarray(cond), "small_dram": small, "pieces_dram": pieces}
    nc = bacc.Bacc("TRN2", target_bir_lowering=False, num_devices=1)
    f = mybir.dt.float32
    args = [nc.dram_tensor(k, v.shape, f, kind="ExternalInput").ap() for k, v in arrays.items()]
    out = nc.dram_tensor(_OUT, (NCH, P, KT * C), f, kind="ExternalOutput").ap()
    cond_resid_kernel(nc, *args, out)
    r = run_bass_kernel_spmd(nc, [arrays], core_ids=[0])
    got = np.asarray(r.results[0][_OUT]).reshape(NCH, P, KT, S, B)
    return np.ascontiguousarray(got.transpose(4, 0, 3, 2, 1).reshape(B, T, D))
```

```python
import concourse.bass as bass
from concourse import mybir
from contextlib import ExitStack

B = 16
T = 512
D = 512
P = 128
KT = D // P
S = 16
C = S * B
NCH = T // S
NG = 4 * D // P
NGIF = 3 * D // P
GIF = NGIF * B
W1 = KT * B
N = 64
TAPS = 16
R = 8
LAG = 5
EPS = 1e-5
PIECE = 4096
HALO = (TAPS - 1) * B

SMALL = {}
_at = 0
for _name, _n in (("cond", W1), ("b0", NG), ("conv_b", KT), ("bo", KT), ("b3", KT), ("b1", KT), ("ln_g", KT),
                  ("ln_b", KT), ("b2", 2 * KT * R), ("alpha", W1), ("bp", 1), ("bs", 1), ("a_dt", 2),
                  ("mask", C), ("ident", P)):
    SMALL[_name] = slice(_at, _at + _n)
    _at += _n
NSMALL = _at

DVE_VAR, DVE_NORM = 3, 5
DVE_AE = DVE_NORM + KT
DVE_LORA = 22
SETUP_DVE = DVE_LORA + 4 * KT + 2 * KT + 2
PE_HIDDEN = 2
K_DVE = 2
CONV_OPS = TAPS * K_DVE
CONV_PRODS = TAPS * (KT - K_DVE)
CONV_ADDS = (TAPS - 1) * (KT - K_DVE)
PRODS_PER = 4
RING = 2
CONV_PER = 4
SCAN_OPS = 9
SCAN_AT = 11
XW_FIRST = 0
XW_HALVES = (4, 1, 1, 1, 1, 1, 3, 3, 3, 2, 4, 3, 3, 2, 0, 0)
X_SPLIT_AT = 14
XW_AT, _at = [], 0
for _n in XW_HALVES:
    XW_AT.append([divmod(h, 2) for h in range(_at, _at + _n)])
    _at += _n
assert _at == 2 * NG


def lora_read(t):
    return DVE_LORA + (4 * t if t < KT else 2 * KT + 2 * t) + 2


N_PIECES = 7 + 2 * KT


def cond_resid_kernel(nc, xT, cond_row, small, pieces, outT):
    f32 = mybir.dt.float32
    bf16 = mybir.dt.bfloat16
    ALU = mybir.AluOpType
    ACT = mybir.ActivationFunctionType

    ctx = ExitStack()
    with ctx:
        def sb(name, cols, dt=f32, parts=P):
            return ctx.enter_context(nc.sbuf_tensor(name, [parts, cols], dt))

        def sem(name):
            return ctx.enter_context(nc.semaphore(name))

        wh = [sb(f"wh_{p}", KT * 4 * D, bf16) for p in ("hi", "lo")]
        wx = [sb(f"wx_{p}", KT * 4 * D, bf16) for p in ("hi", "lo")]
        m1 = [sb(f"base_wz_{p}", 2 * KT * D, bf16) for p in ("hi", "lo")]
        m2 = [sb(f"wg_wp_ws_wo_{p}", PIECE, bf16) for p in ("hi", "lo")]
        lra = [sb(f"lora_a_{p}", KT * P, bf16) for p in ("hi", "lo")]
        lrb = [sb(f"lora_b_{p}", D, bf16) for p in ("hi", "lo")]

        def whs(p, kt, ft):
            return wh[p][:, (kt * NG + ft) * P:(kt * NG + ft + 1) * P]

        def wxs(p, kt, ft):
            return wx[p][:, (kt * NG + ft) * P:(kt * NG + ft + 1) * P]

        def bases(p, kt, ot):
            return m1[p][:, kt * D + ot * P:kt * D + (ot + 1) * P]

        def wzs(p, kt, ot):
            return m1[p][:, (KT + kt) * D + ot * P:(KT + kt) * D + (ot + 1) * P]

        def wgs(p, kt, ot):
            return m2[p][:, kt * D + ot * P:kt * D + (ot + 1) * P]

        def wps(p, kt):
            return m2[p][:, KT * D + kt * P:KT * D + (kt + 1) * P]

        def wss(p, kt):
            return m2[p][:, KT * D + D + kt * P:KT * D + D + (kt + 1) * P]

        def wos(p, ot):
            return m2[p][0:N, KT * D + 2 * D + ot * P:KT * D + 2 * D + (ot + 1) * P]

        sp = sb("small_params", NSMALL)

        def par(name, k=None):
            a = SMALL[name]
            return sp[:, a] if k is None else sp[:, a.start + k:a.start + k + 1]

        leak = sb("leak", W1)
        ssm = sb("ssm_params", 8, parts=N)
        decay_t = sb("decay_tile", C, parts=N)

        xw = sb("xw", 2 * S * NG * B)
        x_in = sb("x_in", KT * C)
        x_s = [sb(f"x_{p}", KT * C, bf16) for p in ("hi", "lo")]
        x_res = sb("x_res", KT * C)
        x1 = sb("x1", KT * C)
        win = sb("win", KT * (HALO + C))
        conv = sb("conv", KT * C)
        conv_s = [sb(f"conv_{p}", KT * C, bf16) for p in ("hi", "lo")]
        win_s = conv_s
        x2, x2_s = conv, conv_s
        x3_s = [sb(f"x3_{p}", KT * C, bf16) for p in ("hi", "lo")]
        z3 = sb("z3", 2 * S * W1)
        zw3 = sb("zw3", 2 * S * W1)
        outb = sb("outb", KT * C)
        prod = sb("conv_products", RING * C)
        gsum = sb("gate_sums", NG * B)
        fi = sb("sig_f_i", 2 * W1)
        cg = sb("c_and_g", 2 * W1)
        fcig = sb("fc_ig", 2 * W1)
        so = sb("sig_o", W1)
        tc = sb("tanh_c", W1)
        h0 = sb("h0", W1)
        h0_s = sb("h0_split", 2 * W1, bf16)
        s3 = sb("l3_sums", W1)
        gate3 = sb("l3_gate", W1)
        gz = sb("l3_gz", W1)
        hl = sb("l3_h_leak", W1)
        pre3 = sb("l3_pre", W1)
        h3 = sb("l3_h", W1)
        h3_s = sb("l3_h_split", 2 * W1, bf16)
        spa = sb("sp_terms", C, parts=N)
        spe = spl = spa
        spr = sb("sp_relu", C, parts=N)
        bt = bu = spr
        ct = sb("c_t", C, parts=N)
        vbt = sb("v_bt", C, parts=N)
        state = sb("state", C, parts=N)
        y = vbt
        y_s = [sb(f"y_{p}", C, bf16, parts=N) for p in ("hi", "lo")]
        vm = prod[:, 0:C]
        v_s = [sb(f"lora_v_{p}", C, bf16) for p in ("hi", "lo")]
        crow = outb[0:B, 0:D]
        stats = sb("ln_stats", 16, parts=B)
        ae = x1
        hid = x2
        w2_s = [conv_s, x3_s]
        hid_s = v_s[0][:, 0:2 * W1]
        lrt = z3

        def pb(name):
            return ctx.enter_context(nc.psum_tensor(name, [P, 512], f32))

        p_gif, p_o, p_l3, p_x0, p_x1, p_m0, p_m1, p_p = (
            pb(n) for n in ("p_gif", "p_o", "p_l3", "p_x0", "p_x1", "p_m0", "p_m1", "p_proj"))
        p_x = [p_x0, p_x1]
        p_m = [p_m0, p_m1]

        small_in, piece_in = sem("small_in"), [sem("piece_in_even"), sem("piece_in_odd")]
        piece_hi, piece_split = sem("piece_hi"), sem("piece_split")
        w2_hi, w2_lo, w2_mm = sem("w2_hi"), sem("w2_lo"), sem("w2_mm")
        x_loaded, res_loaded, out_stored = sem("x_loaded"), sem("res_loaded"), sem("out_stored")
        setup_dve, setup_act, setup_pe = sem("setup_dve"), sem("setup_act"), sem("setup_pe")
        x_split_hi, x_split_lo = sem("x_split_hi"), sem("x_split_lo")
        xw_mm, xw_done = sem("xw_mm"), sem("xw_done")
        gif_mm, o_mm = sem("gif_mm"), sem("o_mm")
        gif_part, gif_sum, o_part, o_sum = sem("gif_part"), sem("gif_sum"), sem("o_part"), sem("o_sum")
        g_tanh, fi_sig, o_sig, c_tanh = sem("g_tanh"), sem("fi_sig"), sem("o_sig"), sem("c_tanh")
        fcig_done, c_new, h0_f32, h0_split, x1_done = (sem(n) for n in ("fcig_done", "c_new", "h0_f32", "h0_split", "x1_done"))
        win_moved, win_hi, win_lo, u_mm, conv_op, conv_hi, conv_lo, proj_mm = (
            sem(n) for n in ("win_moved", "win_hi", "win_lo", "u_mm", "conv_op", "conv_hi", "conv_lo", "proj_mm"))
        conv_prod, conv_add = sem("conv_prod"), sem("conv_add")
        sp_abs, c_done, sp_exp, sp_log, scan_op, wo_mm, x2_done, x2_hi, x2_lo = (
            sem(n) for n in ("sp_abs_done", "c_done", "sp_exp_done", "sp_log_done", "scan_op", "wo_mm", "x2_done",
                             "x2_hi_done", "x2_lo_done"))
        v_mm, v_op, l2_mm, x3_done, x3_hi, x3_lo, zw_mm, zw_done = (
            sem(n) for n in ("v_mm", "v_op", "l2_mm", "x3_done", "x3_hi_done", "x3_lo_done", "zw_mm", "zw_done"))
        l3_mm, s3_part, s3_sum, l3_gate, l3_gz, l3_pre, l3_h, l3_split, l3_leak, l3_out = (
            sem(n) for n in ("l3_mm", "s3_part", "s3_sum", "l3_gate_done", "l3_gz_done", "l3_pre_done", "l3_h_done",
                             "l3_split", "l3_leak_done", "l3_out_done"))

        def kb(t, lo, n=W1):
            return t[:, lo:lo + n].rearrange("p (k b) -> p k b", b=B)

        def step_cols(t, s):
            return t[:, :].rearrange("p (k c) -> p k c", k=KT)[:, :, s * B:(s + 1) * B]

        def tile(t, k):
            return t[:, k * C:(k + 1) * C]

        def xw_slots(p):
            return xw[:, p * S * NG * B:(p + 1) * S * NG * B].rearrange("p (t g) -> p t g", t=S)

        def xw_step(p, s):
            return xw[:, (p * S + s) * NG * B:(p * S + s + 1) * NG * B].rearrange("p (g b) -> p g b", b=B)

        def by_step(t, p):
            return t[:, p * S * W1:(p + 1) * S * W1].rearrange("p (t k b) -> p k t b", k=KT, b=B)

        def l3_step(t, p, s, dims=True):
            q = p if s >= LAG else 1 - p
            v = t[:, (q * S + (s - LAG) % S) * W1:(q * S + (s - LAG) % S + 1) * W1]
            return v.rearrange("p (k b) -> p k b", b=B) if dims else v

        def as_kt(t):
            return t[:, :].rearrange("p (k t b) -> p k t b", k=KT, b=B)

        win_v = win[:, :].rearrange("p (k c) -> p k c", k=KT)
        x1_v = x1[:, :].rearrange("p (k c) -> p k c", k=KT)
        h0_v = h0_s[:, :].rearrange("p (k q b) -> p k q b", q=2, b=B)
        hid_v = hid_s.rearrange("p (k q b) -> p k q b", q=2, b=B)
        h3_v = h3_s[:, :].rearrange("p (k q b) -> p k q b", q=2, b=B)

        places = [(wh, 0), (wh, PIECE), (wx, 0), (wx, PIECE), (m1, 0), (m2, 0)]

        def w2_part(t, k):
            at = ((7 + t) % 2) * PIECE + k * R * P
            return xw[:, at:at + R * P]

        block = ctx.enter_context(nc.Block())

        def has_l0(c):
            return not isinstance(c, int) or c < NCH

        def has_mid(c):
            return not isinstance(c, int) or 1 <= c <= NCH

        def has_z(c):
            return not isinstance(c, int) or 2 <= c <= NCH + 1

        def has_l3(c, s):
            return not isinstance(c, int) or 0 <= S * (c - 2) + s - LAG < T

        def iterations(engine, body):
            for c in range(4):
                body(c, c % 2)
            with engine.Fori(4, NCH - 1, 2) as c:
                body(c, 0)
                body(c + 1, 1)
            for c in range(NCH, NCH + 3):
                body(c, c % 2)

        @block.sync
        def _(sync):
            sync.dma_start(sp[:, :], small).then_inc(small_in, 16)
            sync.dma_start(crow, cond_row).then_inc(small_in, 16)
            sync.dma_start(x_in[:, :], xT[0, :, :]).then_inc(x_loaded, 16)
            for n in range(N_PIECES):
                if 2 <= n < 8:
                    sync.wait_ge(piece_split, n - 1)
                elif n == 8:
                    sync.wait_ge(setup_pe, PE_HIDDEN)
                elif n > 8:
                    sync.wait_ge(w2_lo, KT * (n - 8))
                sync.dma_start(xw[:, (n % 2) * PIECE:(n % 2 + 1) * PIECE], pieces[n, :, :]).then_inc(piece_in[n % 2], 16)

            sync.wait_ge(x_split_hi, 1)
            sync.wait_ge(x_split_lo, 1)
            sync.dma_start(x_in[:, :], xT[1, :, :]).then_inc(x_loaded, 16)

            def body(c, p):
                if has_l0(c):
                    sync.wait_ge(x_split_hi, c + 2)
                    sync.wait_ge(x_split_lo, c + 2)
                    sync.dma_start(x_in[:, :], xT[c + 2, :, :]).then_inc(x_loaded, 16)
                    if not (isinstance(c, int) and c == 0):
                        sync.wait_ge(x1_done, S * c)
                    sync.dma_start(x_res[:, :], xT[c, :, :]).then_inc(res_loaded, 16)
                if not isinstance(c, int) or c >= 3:
                    sync.wait_ge(l3_out, S * (c - 2))
                    sync.dma_start(outT[c - 3, :, :], outb[:, :]).then_inc(out_stored, 16)

            iterations(sync, body)
            sync.wait_ge(out_stored, 16 * NCH)
            sync.wait_ge(x_loaded, 16 * (NCH + 2))

        @block.gpsimd
        def _(pool):
            def low(dst, src, hi, done, ready, n):
                pool.wait_ge(ready, n)
                nc.gpsimd.tensor_tensor(dst, src, hi, ALU.subtract).then_inc(done, 1)

            def conv_adds(c, taps):
                for n in taps:
                    j, k = divmod(n, KT - K_DVE)
                    if j == 0:
                        continue
                    a = n - (KT - K_DVE)
                    pool.wait_ge(conv_prod, CONV_PRODS * (c - 1) + n + 1)
                    if j > 1:
                        pool.wait_ge(conv_add, CONV_ADDS * (c - 1) + a - (KT - K_DVE) + 1)
                    t = tile(conv, K_DVE + k)
                    nc.gpsimd.tensor_tensor(t, t, prod[:, (n % RING) * C:(n % RING + 1) * C], ALU.add).then_inc(conv_add, 1)

            def splits(c, p, s):
                if s == X_SPLIT_AT + 1 and has_l0(c):
                    low(x_s[1][:, :], x_in[:, :], x_s[0][:, :], x_split_lo, x_split_hi, c + 3)
                if s == 0 and has_z(c):
                    low(as_kt(x3_s[1]), by_step(z3, p), as_kt(x3_s[0]), x3_lo, x3_hi, c - 1)
                if s == 1 and has_mid(c):
                    pool.wait_ge(win_hi, c)
                    nc.gpsimd.tensor_tensor(win_s[1][:, :].rearrange("p (k c) -> p k c", k=KT), win_v[:, :, HALO:],
                                            win_s[0][:, :].rearrange("p (k c) -> p k c", k=KT),
                                            ALU.subtract).then_inc(win_lo, 1)
                if s == 8 and has_mid(c):
                    low(conv_s[1][:, :], conv[:, :], conv_s[0][:, :], conv_lo, conv_hi, c)
                if s == 12 and has_mid(c):
                    low(x2_s[1][:, :], x2[:, :], x2_s[0][:, :], x2_lo, x2_hi, c)
                if has_mid(c):
                    conv_adds(c, range(PRODS_PER * s, min(PRODS_PER * (s + 1), CONV_PRODS)))

            pool.wait_ge(setup_dve, SETUP_DVE)
            nc.gpsimd.tensor_tensor(hl[:, :], h3[:, :], leak[:, :], ALU.mult).then_inc(l3_leak, 1)

            low(x_s[1][:, :], x_in[:, :], x_s[0][:, :], x_split_lo, x_split_hi, 1)
            low(x_s[1][:, :], x_in[:, :], x_s[0][:, :], x_split_lo, x_split_hi, 2)

            def body(c, p):
                m = c - 1
                for s in range(S):
                    g3 = S * (c - 2) + s - LAG
                    if has_l3(c, s):
                        t = (s - LAG) % S
                        if s == LAG and not (isinstance(c, int) and c == 2):
                            pool.wait_ge(out_stored, 16 * (c - 2))
                        pool.wait_ge(l3_h, g3 + 1)
                        nc.gpsimd.tensor_tensor(step_cols(outb, t), l3_step(z3, p, s), kb(h3, 0), ALU.add).then_inc(l3_out, 1)
                        nc.gpsimd.tensor_tensor(hl[:, :], h3[:, :], leak[:, :], ALU.mult).then_inc(l3_leak, 1)
                    splits(c, p, s)

            iterations(pool, body)

        SETUP_ACT = {}

        @block.scalar
        def _(act):
            done = [0]

            def setup(name, ins):
                ins.then_inc(setup_act, 1)
                done[0] += 1
                SETUP_ACT[name] = done[0]

            act.wait_ge(small_in, 32)
            setup("abs", nc.scalar.activation(ssm[:, 3:5], par("a_dt")[0:N, :], ACT.Abs))
            act.wait_ge(setup_act, 1)
            setup("exp", nc.scalar.activation(ssm[:, 5:7], ssm[:, 3:5], ACT.Exp, scale=-1.0))
            act.wait_ge(setup_act, 2)
            setup("log", nc.scalar.activation(ssm[:, 3:5], ssm[:, 5:7], ACT.Ln, bias=1.0))
            act.wait_ge(setup_dve, DVE_VAR)
            setup("std", nc.scalar.activation(stats[:, 9:10], stats[:, 8:9], ACT.Sqrt))
            for n, (dst, at) in enumerate(places):
                act.wait_ge(piece_in[n % 2], 16 * (n // 2 + 1))
                nc.scalar.activation(dst[0][:, at:at + PIECE], xw[:, (n % 2) * PIECE:(n % 2 + 1) * PIECE],
                                     ACT.Copy).then_inc(piece_hi, 1)
            act.wait_ge(setup_pe, 2)
            for it in range(KT):
                setup("gelu", nc.scalar.activation(hid[:, it * B:(it + 1) * B], p_p[:, 64 + it * B:64 + (it + 1) * B],
                                                   ACT.Gelu, bias=par("b1", it)))

            for q in range(2 * KT * KT):
                t, k = divmod(q, KT)
                n = 7 + t
                if k == 0:
                    act.wait_ge(piece_in[n % 2], 16 * (n // 2 + 1))
                if q >= 2:
                    act.wait_ge(w2_mm, q - 1)
                nc.scalar.activation(w2_s[q % 2][0][:, :], w2_part(t, k), ACT.Copy).then_inc(w2_hi, 1)

            def high(dst, src, done, ready, n):
                act.wait_ge(ready, n)
                nc.scalar.activation(dst, src, ACT.Copy).then_inc(done, 1)

            def xw_out(q, par_, ft):
                act.wait_ge(xw_mm, NG * q + ft + 1)
                out = xw_slots(par_)[:, :, ft * B:(ft + 1) * B]
                nc.scalar.activation(out, p_x[ft % 2][:, 0:C].rearrange("p (t b) -> p t b", b=B), ACT.Identity,
                                     bias=par("b0", ft)).then_inc(xw_done, 1)

            high(x_s[0][:, :], x_in[:, :], x_split_hi, x_loaded, 16)
            act.wait_ge(w2_lo, 2 * KT * KT)
            for ft in range(NG):
                xw_out(0, 0, ft)
            high(x_s[0][:, :], x_in[:, :], x_split_hi, x_loaded, 32)

            def conv_products(c, taps):
                for n in taps:
                    j, k = divmod(n, KT - K_DVE)
                    k += K_DVE
                    src = win[:, k * (HALO + C) + j * B:k * (HALO + C) + j * B + C]
                    w = sp[:, SMALL["cond"].start + k * B + j:SMALL["cond"].start + k * B + j + 1]
                    if j == 0:
                        ins = nc.scalar.activation(tile(conv, k), src, ACT.Identity, scale=w, bias=par("conv_b", k))
                    else:
                        if n - RING >= KT - K_DVE:
                            act.wait_ge(conv_add, CONV_ADDS * (c - 1) + n - RING - (KT - K_DVE) + 1)
                        ins = nc.scalar.activation(prod[:, (n % RING) * C:(n % RING + 1) * C], src, ACT.Identity,
                                                   scale=w)
                    ins.then_inc(conv_prod, 1)

            def body(c, p):
                for s in range(S):
                    g = S * c + s
                    g3 = S * (c - 2) + s - LAG
                    prods = range(PRODS_PER * s, min(PRODS_PER * (s + 1), CONV_PRODS)) if has_mid(c) else ()
                    if s == X_SPLIT_AT and has_l0(c):
                        act.wait_ge(xw_mm, NG * (c + 2))
                        high(x_s[0][:, :], x_in[:, :], x_split_hi, x_loaded, 16 * (c + 3))
                    if has_l3(c, s):
                        act.wait_ge(s3_sum, g3 + 1)
                        nc.scalar.activation(gate3[:, :], s3[:, :], ACT.Sigmoid).then_inc(l3_gate, 1)
                        act.wait_ge(l3_pre, g3 + 1)
                        if not (isinstance(c, int) and c == 2 and s == LAG):
                            act.wait_ge(l3_split, 2 * g3 + 2)
                            act.wait_ge(l3_out, g3)
                        act.wait_ge(l3_leak, g3 + 1)
                        nc.scalar.activation(h3[:, :], pre3[:, :], ACT.Tanh).then_inc(l3_h, 1)
                    if s == 12 and has_mid(c):
                        high(x2_s[0][:, :], x2[:, :], x2_hi, x2_done, KT * c)
                    if s == 0 and has_z(c):
                        high(as_kt(x3_s[0]), by_step(z3, p), x3_hi, x3_done, KT * (c - 1))
                    if s == 0 and has_mid(c):
                        act.wait_ge(win_moved, 2 * c)
                    conv_products(c, prods[:2])
                    if has_l0(c):
                        act.wait_ge(gif_sum, g + 1)
                        nc.scalar.activation(fi[:, :], gsum[:, W1:3 * W1], ACT.Sigmoid).then_inc(fi_sig, 1)
                        nc.scalar.activation(cg[:, W1:2 * W1], gsum[:, 0:W1], ACT.Tanh).then_inc(g_tanh, 1)
                        act.wait_ge(o_sum, g + 1)
                        nc.scalar.activation(so[:, :], gsum[:, 3 * W1:4 * W1], ACT.Sigmoid).then_inc(o_sig, 1)
                        act.wait_ge(c_new, g + 1)
                        nc.scalar.activation(tc[:, :], cg[:, 0:W1], ACT.Tanh).then_inc(c_tanh, 1)
                    if s == 0 and has_mid(c):
                        act.wait_ge(win_moved, 2 * c)
                        nc.scalar.activation(win_s[0][:, :].rearrange("p (k c) -> p k c", k=KT), win_v[:, :, HALO:],
                                             ACT.Copy).then_inc(win_hi, 1)
                    conv_products(c, prods[2:])
                    if s == 7 and has_mid(c):
                        act.wait_ge(conv_add, CONV_ADDS * c)
                        high(conv_s[0][:, :], conv[:, :], conv_hi, conv_op, CONV_OPS * c)
                    if s == 9 and has_mid(c):
                        act.wait_ge(proj_mm, c)
                        nc.scalar.activation(spa[:, :], p_p[0:N, 0:C], ACT.Abs, bias=par("bp")[0:N, :]).then_inc(sp_abs, 1)
                        nc.scalar.activation(ct[:, :], p_p[N:P, 0:C], ACT.Tanh, bias=par("bp")[N:P, :]).then_inc(c_done, 1)
                    if s == 10 and has_mid(c):
                        nc.scalar.preload_act_table_set("natural_log_exp_and_others")
                        act.wait_ge(sp_abs, c)
                        nc.scalar.activation(spe[:, :], spa[:, :], ACT.Exp, scale=-1.0).then_inc(sp_exp, 1)
                        act.wait_ge(sp_exp, c)
                        nc.scalar.activation(spl[:, :], spe[:, :], ACT.Ln, bias=1.0).then_inc(sp_log, 1)
                        nc.scalar.preload_act_table_set("sigmoid_and_others")
                    if s in (2, 4) and has_z(c):
                        for ot in (s - 2, s - 1):
                            act.wait_ge(zw_mm, KT * (c - 2) + s)
                            nc.scalar.activation(by_step(zw3, p)[:, ot], p_m[ot // 2][:, (ot % 2) * C:(ot % 2 + 1) * C]
                                                 .rearrange("p (t b) -> p t b", b=B), ACT.Identity,
                                                 bias=par("b3", ot)).then_inc(zw_done, 1)
                    if has_l0(c):
                        for ft, half in XW_AT[s]:
                            if half == 1:
                                xw_out(c + 1, 1 - p, ft)

            iterations(act, body)

        @block.tensor
        def _(pe):
            mm = nc.tensor.matmul

            def three(out, ws, xs, kts, first, last):
                todo = [(k, a, b) for k in kts for a, b in ((0, 0), (0, 1), (1, 0))]
                ins = None
                for n, (k, a, b) in enumerate(todo):
                    ins = mm(out, ws(a, k), xs(b, k), start=first and n == 0, stop=last and n == len(todo) - 1)
                return ins

            pe.wait_ge(setup_dve, DVE_NORM)
            for k in range(KT):
                ins = nc.tensor.transpose(p_p[:, k * B:(k + 1) * B], outb[0:B, k * P:(k + 1) * P], par("ident")[0:B, 0:B])
            ins.then_inc(setup_pe, 1)
            pe.wait_ge(piece_in[0], 16 * 4)
            pe.wait_ge(setup_dve, DVE_AE)
            for it in range(KT):
                for k in range(KT):
                    ins = mm(p_p[:, 64 + it * B:64 + (it + 1) * B], xw[:, k * D + it * P:k * D + (it + 1) * P],
                             ae[:, k * B:(k + 1) * B], start=k == 0, stop=k == KT - 1)
            ins.then_inc(setup_pe, 1)
            pe.wait_ge(setup_dve, DVE_LORA)
            for t in range(2 * KT):
                if t >= 2:
                    pe.wait_ge(setup_dve, lora_read(t - 2))
                for k in range(KT):
                    q = t * KT + k
                    pe.wait_ge(w2_hi, q + 1)
                    pe.wait_ge(w2_lo, q + 1)
                    for r in range(R):
                        mm(p_m[t % 2][:, r * 2 * B:(r + 1) * 2 * B], w2_s[q % 2][0][:, r * P:(r + 1) * P],
                           hid_s[:, k * 2 * B:(k + 1) * 2 * B], start=r == 0 and k == 0, stop=False,
                           skip_group_check=True)
                    for r in range(R):
                        ins = mm(p_m[t % 2][:, r * 2 * B:r * 2 * B + B], w2_s[q % 2][1][:, r * P:(r + 1) * P],
                                 hid_s[:, k * 2 * B:k * 2 * B + B], start=False, stop=k == KT - 1 and r == R - 1,
                                 skip_group_check=True)
                    ins.then_inc(w2_mm, 1)
            pe.wait_ge(setup_dve, lora_read(2 * KT - 1))
            for t in range(KT):
                ins = nc.tensor.transpose(p_p[:, t * P:(t + 1) * P], lrt[:, t * P:(t + 1) * P], par("ident"))
            ins.then_inc(setup_pe, 1)

            def xw_products(q, ft, half):
                if half == 0 and not (isinstance(q, int) and q == 0 and ft < 2):
                    pe.wait_ge(xw_done, NG * q + ft - 1)
                ins = three(p_x[ft % 2][:, 0:C], lambda a, k: wxs(a, k, ft), lambda b, k: tile(x_s[b], k),
                            (2 * half, 2 * half + 1), half == 0, half == 1)
                if half == 1:
                    ins.then_inc(xw_mm, 1)

            def gate_products(bank, fts, wait_low):
                for n, ft in enumerate(fts):
                    for k in range(KT):
                        mm(bank[:, n * 2 * B:n * 2 * B + B], whs(1, k, ft), h0_s[:, k * 2 * B:k * 2 * B + B],
                           start=n == 0 and k == 0, stop=False, skip_group_check=True)
                if wait_low is not None:
                    pe.wait_ge(h0_split, wait_low)
                for n, ft in enumerate(fts):
                    for k in range(KT):
                        ins = mm(bank[:, n * 2 * B:(n + 1) * 2 * B], whs(0, k, ft), h0_s[:, k * 2 * B:(k + 1) * 2 * B],
                                 start=False, stop=ft == fts[-1] and k == KT - 1, skip_group_check=True)
                return ins

            def lstm_products(c, s):
                g = S * c + s
                pe.wait_ge(h0_split, 2 * g + 1)
                gate_products(p_gif, range(NGIF), 2 * g + 2).then_inc(gif_mm, 1)
                gate_products(p_o, range(NGIF, NG), None).then_inc(o_mm, 1)

            def l3_products(g3):
                pe.wait_ge(l3_split, 2 * g3 + 2)
                for ot in range(KT):
                    for k in range(KT):
                        mm(p_l3[:, ot * 2 * B:(ot + 1) * 2 * B], wgs(0, k, ot), h3_s[:, k * 2 * B:(k + 1) * 2 * B],
                           start=k == 0, stop=False)
                    for k in range(KT):
                        ins = mm(p_l3[:, ot * 2 * B:ot * 2 * B + B], wgs(1, k, ot), h3_s[:, k * 2 * B:k * 2 * B + B],
                                 start=False, stop=k == KT - 1)
                ins.then_inc(l3_mm, 1)

            pe.wait_ge(piece_split, 6)
            pe.wait_ge(setup_dve, SETUP_DVE)
            pe.wait_ge(x_split_hi, 1)
            pe.wait_ge(x_split_lo, 1)
            for ft in range(NG):
                for half in (0, 1):
                    xw_products(0, ft, half)

            def body(c, p):
                for s in range(S):
                    if has_l3(c, s):
                        l3_products(S * (c - 2) + s - LAG)
                    if has_l0(c):
                        lstm_products(c, s)
                    if has_l0(c) and XW_AT[s]:
                        if s == XW_FIRST:
                            pe.wait_ge(x_split_hi, c + 2)
                            pe.wait_ge(x_split_lo, c + 2)
                        for ft, half in XW_AT[s]:
                            xw_products(c + 1, ft, half)
                    if s in (1, 2, 3, 4) and has_z(c):
                        if s == 1:
                            pe.wait_ge(x3_hi, c - 1)
                            pe.wait_ge(x3_lo, c - 1)
                        for ot in (s - 1,):
                            three(p_m[ot // 2][:, (ot % 2) * C:(ot % 2 + 1) * C], lambda a, k: wzs(a, k, ot),
                                  lambda b, k: tile(x3_s[b], k), range(KT), True, True).then_inc(zw_mm, 1)
                    if s == 5 and has_mid(c):
                        pe.wait_ge(win_hi, c)
                        pe.wait_ge(win_lo, c)
                        three(p_p[:, C:2 * C], lambda a, k: wss(a, k), lambda b, k: tile(win_s[b], k), range(KT),
                              True, True).then_inc(u_mm, 1)
                    if s == 9 and has_mid(c):
                        pe.wait_ge(conv_hi, c)
                        pe.wait_ge(conv_lo, c)
                        three(p_p[:, 0:C], lambda a, k: wps(a, k), lambda b, k: tile(conv_s[b], k), range(KT),
                              True, True).then_inc(proj_mm, 1)
                    if s == 11 and has_mid(c):
                        pe.wait_ge(scan_op, SCAN_OPS * c)
                        for ot in range(KT):
                            three(p_m[ot // 2][:, (ot % 2) * C:(ot % 2 + 1) * C], lambda a, k: wos(a, ot),
                                  lambda b, k: y_s[b][:, :], (0,), True, True).then_inc(wo_mm, 1)
                    if s == 13 and has_mid(c):
                        pe.wait_ge(x2_hi, c)
                        pe.wait_ge(x2_lo, c)
                        three(p_p[:, 0:C], lambda a, k: lra[a][:, k * P:(k + 1) * P], lambda b, k: tile(x2_s[b], k),
                              range(KT), True, True).then_inc(v_mm, 1)
                    if s in (14, 15) and has_mid(c):
                        pe.wait_ge(v_op, 3 * c)
                        for ot in (2 * (s - 14), 2 * (s - 14) + 1):
                            out = p_m[ot // 2][:, (ot % 2) * C:(ot % 2 + 1) * C]
                            three(out, lambda a, k: bases(a, k, ot), lambda b, k: tile(x2_s[b], k), range(KT), True, False)
                            three(out, lambda a, k: lrb[a][:, ot * P:(ot + 1) * P], lambda b, k: v_s[b][:, :], (0,),
                                  False, True).then_inc(l2_mm, 1)

            iterations(pe, body)

        @block.vector
        def _(dve):
            tt, ts, stt = nc.vector.tensor_tensor, nc.vector.tensor_scalar, nc.vector.scalar_tensor_tensor
            n_setup = [0]

            def setup(ins):
                ins.then_inc(setup_dve, 1)
                n_setup[0] += 1

            def settled():
                dve.wait_ge(setup_dve, n_setup[0])

            dve.wait_ge(small_in, 32)
            setup(nc.vector.bn_stats(stats[:, 0:6], crow))
            settled()
            setup(nc.vector.bn_aggr(stats[:, 6:8], stats[:, 0:6]))
            settled()
            setup(ts(stats[:, 8:9], stats[:, 7:8], EPS, None, ALU.add))
            assert n_setup[0] == DVE_VAR
            dve.wait_ge(setup_act, SETUP_ACT["std"])
            setup(nc.vector.reciprocal(stats[:, 10:11], stats[:, 9:10]))
            settled()
            setup(ts(crow, crow, stats[:, 6:7], stats[:, 10:11], ALU.subtract, ALU.mult))
            assert n_setup[0] == DVE_NORM
            dve.wait_ge(setup_pe, 1)
            for k in range(KT):
                setup(ts(ae[:, k * B:(k + 1) * B], p_p[:, k * B:(k + 1) * B], par("ln_g", k), par("ln_b", k),
                         ALU.mult, ALU.add))
            assert n_setup[0] == DVE_AE
            setup(stt(ssm[:, 0:2], par("a_dt")[0:N, :], 0.0, ssm[:, 3:5], ALU.max, ALU.add))
            settled()
            setup(tt(ssm[:, 2:3], ssm[:, 0:1], ssm[:, 1:2], ALU.mult))
            setup(nc.vector.memset(decay_t[:, :], 1.0))
            settled()
            setup(ts(ssm[:, 2:3], ssm[:, 2:3], -1.0, 1.0, ALU.mult, ALU.add))
            setup(nc.vector.memset(decay_t[:, :].rearrange("p (b t) -> p b t", t=S)[:, :, 0], 0.0))
            settled()
            setup(ts(decay_t[:, :], decay_t[:, :], ssm[:, 2:3], None, ALU.mult))
            setup(nc.vector.memset(cg[:, :], 0.0))
            setup(nc.vector.memset(win[:, :], 0.0))
            setup(nc.vector.memset(state[:, :], 0.0))
            setup(ts(leak[:, :], par("alpha"), -1.0, 1.0, ALU.mult, ALU.add))
            setup(nc.vector.tensor_copy(h3[:, :], par("cond")))
            for v, done in ((h0_v, h0_split), (h3_v, l3_split)):
                nc.vector.tensor_copy(v[:, :, 0, :], kb(par("cond"), 0)).then_inc(done, 1)
                dve.wait_ge(done, 1)
                tt(v[:, :, 1, :], kb(par("cond"), 0), v[:, :, 0, :], ALU.subtract).then_inc(done, 1)

            for n, (dst, at) in enumerate(places):
                dve.wait_ge(piece_hi, n + 1)
                tt(dst[1][:, at:at + PIECE], xw[:, (n % 2) * PIECE:(n % 2 + 1) * PIECE], dst[0][:, at:at + PIECE],
                   ALU.subtract).then_inc(piece_split, 1)
            dve.wait_ge(setup_act, SETUP_ACT["gelu"])
            setup(nc.vector.tensor_copy(hid_v[:, :, 0, :], kb(hid, 0)))
            settled()
            setup(tt(hid_v[:, :, 1, :], kb(hid, 0), hid_v[:, :, 0, :], ALU.subtract))
            assert n_setup[0] == DVE_LORA, n_setup[0]

            def w2_low(t):
                for q in range(t * KT, (t + 1) * KT):
                    dve.wait_ge(w2_hi, q + 1)
                    tt(w2_s[q % 2][1][:, :], w2_part(t, q % KT), w2_s[q % 2][0][:, :], ALU.subtract).then_inc(w2_lo, 1)

            def low_rank_tile(t):
                dve.wait_ge(w2_mm, KT * (t + 1))
                settled()
                b2 = sp[:, SMALL["b2"].start + t * R:SMALL["b2"].start + (t + 1) * R]
                out = lrt[:, (t % KT) * P:(t % KT + 1) * P].rearrange("p (b r) -> p r b", r=R)
                v = p_m[t % 2][:, 0:2 * P].rearrange("p (r q b) -> p r q b", q=2, b=B)
                setup(tt(out, v[:, :, 1, :], b2.unsqueeze(2).to_broadcast([P, R, B]), ALU.add))
                settled()
                setup(tt(out, v[:, :, 0, :], out, ALU.add))
                settled()
                if t < KT:
                    a = lra[0][:, t * P:(t + 1) * P]
                    setup(nc.vector.tensor_copy(a, lrt[:, t * P:(t + 1) * P]))
                    settled()
                    setup(tt(lra[1][:, t * P:(t + 1) * P], lrt[:, t * P:(t + 1) * P], a, ALU.subtract))

            for t in range(2 * KT):
                w2_low(t)
                if t >= 1:
                    low_rank_tile(t - 1)
            low_rank_tile(2 * KT - 1)
            dve.wait_ge(setup_pe, PE_HIDDEN + 1)
            setup(nc.vector.tensor_copy(lrb[0][:, :], p_p[:, :]))
            settled()
            setup(tt(lrb[1][:, :], p_p[:, :], lrb[0][:, :], ALU.subtract))
            assert n_setup[0] == SETUP_DVE, n_setup[0]
            settled()

            def conv_tap(c, n):
                j, k = divmod(n, K_DVE)
                base = CONV_OPS * (c - 1)
                src = win[:, k * (HALO + C) + j * B:k * (HALO + C) + j * B + C]
                w = sp[:, SMALL["cond"].start + k * B + j:SMALL["cond"].start + k * B + j + 1]
                if j == 0:
                    ins = ts(tile(conv, k), src, w, par("conv_b", k), ALU.mult, ALU.add)
                else:
                    dve.wait_ge(conv_op, base + n - K_DVE + 1)
                    ins = stt(tile(conv, k), src, w, tile(conv, k), ALU.mult, ALU.add)
                ins.then_inc(conv_op, 1)

            def split_h3(g3):
                dve.wait_ge(l3_h, g3 + 1)
                nc.vector.tensor_copy(h3_v[:, :, 0, :], kb(h3, 0)).then_inc(l3_split, 1)
                dve.wait_ge(l3_split, 2 * g3 + 3)
                tt(h3_v[:, :, 1, :], kb(h3, 0), h3_v[:, :, 0, :], ALU.subtract).then_inc(l3_split, 1)

            def lstm_step(c, p, s):
                g = S * c + s
                dve.wait_ge(gif_mm, g + 1)
                if s == 0:
                    dve.wait_ge(xw_done, NG * (c + 1))
                    dve.wait_ge(res_loaded, 16 * (c + 1))
                lo = p_gif[:, 0:2 * GIF].rearrange("p (k q b) -> p k q b", q=2, b=B)
                tt(kb(gsum, 0, GIF), lo[:, :, 1, :], xw_step(p, s)[:, 0:NGIF, :], ALU.add).then_inc(gif_part, 1)
                dve.wait_ge(gif_part, g + 1)
                tt(kb(gsum, 0, GIF), lo[:, :, 0, :], kb(gsum, 0, GIF), ALU.add).then_inc(gif_sum, 1)
                dve.wait_ge(o_mm, g + 1)
                lo = p_o[:, 0:2 * W1].rearrange("p (k q b) -> p k q b", q=2, b=B)
                tt(kb(gsum, GIF), lo[:, :, 1, :], xw_step(p, s)[:, NGIF:NG, :], ALU.add).then_inc(o_part, 1)
                dve.wait_ge(o_part, g + 1)
                tt(kb(gsum, GIF), lo[:, :, 0, :], kb(gsum, GIF), ALU.add).then_inc(o_sum, 1)
                dve.wait_ge(g_tanh, g + 1)
                dve.wait_ge(fi_sig, g + 1)
                tt(fcig[:, :], fi[:, :], cg[:, :], ALU.mult).then_inc(fcig_done, 1)
                dve.wait_ge(fcig_done, g + 1)
                tt(cg[:, 0:W1], fcig[:, 0:W1], fcig[:, W1:2 * W1], ALU.add).then_inc(c_new, 1)
                if has_l3(c, s) and s != SCAN_AT:
                    split_h3(S * (c - 2) + s - LAG)
                dve.wait_ge(o_sig, g + 1)
                dve.wait_ge(c_tanh, g + 1)
                tt(h0_v[:, :, 0, :], kb(so, 0), kb(tc, 0), ALU.mult).then_inc(h0_split, 1)
                tt(h0[:, :], so[:, :], tc[:, :], ALU.mult).then_inc(h0_f32, 1)
                dve.wait_ge(h0_f32, g + 1)
                dve.wait_ge(h0_split, 2 * g + 3)
                tt(h0_v[:, :, 1, :], kb(h0, 0), h0_v[:, :, 0, :], ALU.subtract).then_inc(h0_split, 1)
                tt(step_cols(x1, s), step_cols(x_res, s), kb(h0, 0), ALU.add).then_inc(x1_done, 1)

            def scan_ops(c, ops):
                q = SCAN_OPS * (c - 1)
                by_time = lambda t: t[:, :].rearrange("p (b t) -> p t b", t=S)
                by_batch = lambda t: t[:, :].rearrange("p (t b) -> p t b", b=B)
                for n in ops:
                    if n:
                        dve.wait_ge(scan_op, q + n)
                    if n == 0:
                        dve.wait_ge(sp_abs, c)
                        dve.wait_ge(c_done, c)
                        ins = ts(spr[:, :], p_p[0:N, 0:C], par("bp")[0:N, :], 0.0, ALU.add, ALU.max)
                    elif n == 1:
                        dve.wait_ge(sp_log, c)
                        ins = tt(bt[:, :], spr[:, :], spl[:, :], ALU.add)
                    elif n == 2:
                        dve.wait_ge(u_mm, c)
                        ins = stt(bu[:, :], p_p[0:N, C:2 * C], par("bs")[0:N, :], bt[:, :], ALU.add, ALU.mult)
                    elif n == 3:
                        ins = ts(by_time(vbt), by_batch(bu), ssm[:, 1:2], None, ALU.mult)
                    elif n == 4:
                        first = vbt[:, :].rearrange("p (b t) -> p b t", t=S)[:, :, 0]
                        last = state[:, :].rearrange("p (b t) -> p b t", t=S)[:, :, S - 1]
                        ins = stt(first, last, ssm[:, 2:3], first, ALU.mult, ALU.add)
                    elif n == 5:
                        ins = nc.vector.tensor_tensor_scan(state[:, :], decay_t[:, :], vbt[:, :], 0.0, ALU.mult, ALU.add)
                    elif n == 6:
                        ins = tt(by_batch(y), by_time(state), by_batch(ct), ALU.mult)
                    elif n == 7:
                        ins = nc.vector.tensor_copy(y_s[0][:, :], y[:, :])
                    else:
                        ins = tt(y_s[1][:, :], y[:, :], y_s[0][:, :], ALU.subtract)
                    ins.then_inc(scan_op, 1)

            def x2_tile(c, ot):
                dve.wait_ge(wo_mm, KT * c)
                win_k = win[:, ot * (HALO + C) + HALO:(ot + 1) * (HALO + C)]
                stt(tile(x2, ot), p_m[ot // 2][:, (ot % 2) * C:(ot % 2 + 1) * C], par("bo", ot), win_k,
                    ALU.add, ALU.add).then_inc(x2_done, 1)

            def x3_tile(m, p, ot):
                dve.wait_ge(l2_mm, KT * m + 2 * (ot // 2) + 2)
                stt(by_step(z3, p)[:, ot], tile(x2, ot).rearrange("p (t b) -> p t b", b=B), 2.0,
                    p_m[ot // 2][:, (ot % 2) * C:(ot % 2 + 1) * C].rearrange("p (t b) -> p t b", b=B),
                    ALU.mult, ALU.add).then_inc(x3_done, 1)

            START, SUMMED, PRE, BEFORE, END = range(5)

            def side_work(c, p, s, place):
                if has_z(c):
                    if (s, place) == (LAG, START):
                        dve.wait_ge(zw_done, KT * (c - 1))
                        dve.wait_ge(x3_done, KT * (c - 1))
                    if (s, place) == (0, START):
                        x3_tile(c - 2, p, 2)
                    if (s, place) == (0, SUMMED):
                        x3_tile(c - 2, p, 3)
                if has_mid(c):
                    if (s, place) == (0, SUMMED):
                        dve.wait_ge(x1_done, S * c)
                        if not (isinstance(c, int) and c == 1):
                            dve.wait_ge(win_lo, c - 1)
                            dve.wait_ge(conv_op, CONV_OPS * (c - 1))
                            dve.wait_ge(conv_add, CONV_ADDS * (c - 1))
                        nc.vector.tensor_copy(win_v[:, :, 0:HALO], win_v[:, :, C:C + HALO]).then_inc(win_moved, 1)
                    if (s, place) == (0, PRE):
                        dve.wait_ge(win_moved, 2 * c - 1)
                        nc.vector.tensor_copy(win_v[:, :, HALO:HALO + C], x1_v).then_inc(win_moved, 1)
                        dve.wait_ge(win_moved, 2 * c)
                    if s == 0 and place in (BEFORE, END):
                        taps = (0, 1) if place == BEFORE else (2, 3)
                    else:
                        taps = (CONV_PER * s + place - SUMMED,) if s > 0 and SUMMED <= place <= END else ()
                    for n in taps:
                        if n < CONV_OPS:
                            conv_tap(c, n)
                    if s == 10 and place in (PRE, END):
                        scan_ops(c, (0,) if place == PRE else (1,))
                    if s == SCAN_AT and place in (SUMMED, PRE, BEFORE):
                        scan_ops(c, {SUMMED: (2, 3), PRE: (4, 5), BEFORE: (6, 7, 8)}[place])
                    if (s, place) == (11, END):
                        x2_tile(c, 0)
                    if s == 12 and place in (SUMMED, PRE, BEFORE):
                        x2_tile(c, place - SUMMED + 1)
                    if s == 14 and place in (START, SUMMED, PRE):
                        base = 3 * (c - 1)
                        if place == START:
                            dve.wait_ge(v_mm, c)
                            ins = tt(vm, p_p[:, 0:C], par("mask"), ALU.mult)
                        elif place == SUMMED:
                            dve.wait_ge(v_op, base + 1)
                            ins = nc.vector.tensor_copy(v_s[0][:, :], vm)
                        else:
                            dve.wait_ge(v_op, base + 2)
                            ins = tt(v_s[1][:, :], vm, v_s[0][:, :], ALU.subtract)
                        ins.then_inc(v_op, 1)
                    if s == 15 and place in (SUMMED, PRE):
                        if place == SUMMED and not (isinstance(c, int) and c < 3):
                            dve.wait_ge(l3_out, S * (c - 2))
                            dve.wait_ge(x3_lo, c - 2)
                        x3_tile(c - 1, 1 - p, place - SUMMED)

            def body(c, p):
                for s in range(S):
                    g3 = S * (c - 2) + s - LAG
                    t = (s - LAG) % S
                    side_work(c, p, s, START)
                    if has_l3(c, s):
                        dve.wait_ge(l3_mm, g3 + 1)
                        v = p_l3[:, 0:2 * W1].rearrange("p (k q b) -> p k q b", q=2, b=B)
                        tt(kb(s3, 0), v[:, :, 1, :], l3_step(zw3, p, s), ALU.add).then_inc(s3_part, 1)
                        dve.wait_ge(s3_part, g3 + 1)
                        tt(kb(s3, 0), v[:, :, 0, :], kb(s3, 0), ALU.add).then_inc(s3_sum, 1)
                    side_work(c, p, s, SUMMED)
                    if has_l3(c, s):
                        dve.wait_ge(l3_gate, g3 + 1)
                        tt(gz[:, :], gate3[:, :], l3_step(z3, p, s, False), ALU.mult).then_inc(l3_gz, 1)
                        dve.wait_ge(l3_gz, g3 + 1)
                        dve.wait_ge(l3_leak, g3 + 1)
                        tt(pre3[:, :], gz[:, :], hl[:, :], ALU.add).then_inc(l3_pre, 1)
                    side_work(c, p, s, PRE)
                    if has_l3(c, s) and (s == SCAN_AT or not has_l0(c)):
                        split_h3(g3)
                    side_work(c, p, s, BEFORE)
                    if has_l0(c):
                        lstm_step(c, p, s)
                    side_work(c, p, s, END)

            iterations(dve, body)


_OUT = "out_dram"


def kernel(**inputs):
    import numpy as np
    import concourse.bacc as bacc
    from concourse.bass_utils import run_bass_kernel_spmd

    a = {k: np.asarray(v) for k, v in inputs.items()}
    f32 = np.float32

    def tiles(w):
        return w.reshape(w.shape[0] // P, P, -1).transpose(1, 0, 2).reshape(P, -1)

    def column(v):
        return v.reshape(-1, P).T

    xt = a["x"].reshape(B, NCH, S, KT, P).transpose(1, 4, 3, 2, 0).reshape(NCH, P, KT * C)
    xt = np.concatenate([xt, np.zeros((2, P, KT * C), f32)])

    gates = [3, 1, 0, 2]

    def by_gate(w):
        return np.concatenate([w[..., g * D:(g + 1) * D] for g in gates], axis=-1)

    small = np.zeros((P, NSMALL), f32)

    def put(name, v, rows=slice(0, P)):
        small[rows, SMALL[name]] = v

    cond = a["cond_1024"]
    put("cond", tiles(cond.T))
    put("b0", column(by_gate(a["L0_cond_b"])))
    put("conv_b", column(a["L1_cond_conv_b"]))
    put("bo", column(a["L1_cond_bo"]))
    put("b3", column(a["L3_cond_b"]))
    put("b1", column(a["L2_cond_b1"]))
    put("ln_g", column(a["L2_cond_ln_g"]))
    put("ln_b", column(a["L2_cond_ln_b"]))
    put("b2", a["L2_cond_b2"].reshape(2 * KT, P, R).transpose(1, 0, 2).reshape(P, -1))
    put("alpha", np.repeat(column(a["L3_cond_alpha"]), B, axis=1))
    put("bp", a["L1_cond_bp"].reshape(P, 1))
    put("bs", a["L1_cond_bs"].reshape(N, 1), slice(0, N))
    put("a_dt", np.stack([a["L1_cond_A_log"], a["L1_cond_dt_log"]], axis=1), slice(0, N))
    put("mask", np.tile(np.repeat(np.eye(B, dtype=f32), R, axis=0), (1, S)))
    put("ident", np.eye(P, dtype=f32))

    pieces = np.zeros((N_PIECES, P, PIECE), f32)
    for n, w in ((0, a["L0_cond_Wh"]), (2, a["L0_cond_Wx"])):
        t = tiles(by_gate(w))
        pieces[n], pieces[n + 1] = t[:, :PIECE], t[:, PIECE:]
    w3 = a["L3_cond_W"]
    pieces[4] = np.concatenate([tiles(a["L2_cond_base_layer"]), tiles(w3[:, D:].T)], axis=1)
    ws = a["L1_cond_Ws"]
    pieces[5, :, :KT * D + 2 * D] = np.concatenate(
        [tiles(w3[:, :D].T), tiles(a["L1_cond_Wp"]), tiles(np.concatenate([ws, ws], axis=1))], axis=1)
    pieces[5, :N, KT * D + 2 * D:KT * D + 3 * D] = a["L1_cond_Wo"]
    pieces[6, :, :KT * D] = tiles(a["L2_cond_w1"])
    w2 = a["L2_cond_w2"].reshape(KT, P, 2 * KT, P, R).transpose(2, 1, 0, 4, 3)
    pieces[7:] = w2.reshape(2 * KT, P, PIECE)

    arrays = {"xT_dram": xt, "cond_dram": np.ascontiguousarray(cond), "small_dram": small, "pieces_dram": pieces}
    nc = bacc.Bacc("TRN2", target_bir_lowering=False, num_devices=1)
    f = mybir.dt.float32
    args = [nc.dram_tensor(k, v.shape, f, kind="ExternalInput").ap() for k, v in arrays.items()]
    out = nc.dram_tensor(_OUT, (NCH, P, KT * C), f, kind="ExternalOutput").ap()
    cond_resid_kernel(nc, *args, out)
    r = run_bass_kernel_spmd(nc, [arrays], core_ids=[0])
    got = np.asarray(r.results[0][_OUT]).reshape(NCH, P, KT, S, B)
    return np.ascontiguousarray(got.transpose(4, 0, 3, 2, 1).reshape(B, T, D))
```
